# Optimizing a Trainium2 kernel written in Bass

```python
import numpy as np
import jax
import jax.numpy as jnp

def _softmax(x, axis=-1):
    return jax.nn.softmax(x, axis=axis)

def _gelu(x):
    return jax.nn.gelu(x, approximate=True)

def _silu(x):
    return jax.nn.silu(x)

def _sigmoid(x):
    return jax.nn.sigmoid(x)

def _layernorm(x, axis=-1, eps=1e-05):
    m = jnp.mean(x, axis=axis, keepdims=True)
    v = jnp.var(x, axis=axis, keepdims=True)
    return (x - m) / jnp.sqrt(v + eps)

def _scatter_add(tgt, idx, src, axis=0):
    return tgt.at[idx].add(src)

def _segment_sum(src, seg, n):
    return jax.ops.segment_sum(src, seg, n)
kernel_name = 'mk_gnn_resnorm_d1_gnn_r64_8cc6f9'

def setup_inputs(seed: int=0):
    np.random.seed(seed)
    _w = jnp.asarray

    def _rec_inputs():
        import jax
        import jax.numpy as jnp
        _gk = jax.random.key(seed)
        x = -0.000202 + 1 * jax.random.normal(jax.random.fold_in(_gk, 1), (100000, 128), jnp.float32)
        src = jax.random.randint(jax.random.fold_in(_gk, 2), (50000,), 0, 100000, jnp.int32)
        dst = jnp.minimum((100000 * jax.random.uniform(jax.random.fold_in(_gk, 3), (50000,)) ** 2.0).astype(jnp.int32), 99999)
        _o = jnp.argsort(dst, stable=True)
        src = src[_o]
        dst = dst[_o]
        edge_attr_20 = -8.62073e-06 + 0.999901 * jax.random.normal(jax.random.fold_in(_gk, 12), (50000, 20), jnp.float32)
        edge_weight = jax.random.uniform(jax.random.fold_in(_gk, 13), (50000,), jnp.float32, 0.0, 0.999999)
        return (x, src, dst, edge_attr_20, edge_weight)
    x, src, dst, edge_attr_20, edge_weight = _rec_inputs()

    def _L0_gnn_setup():
        import jax, jax.numpy as jnp
        import numpy as np
        N_ATOMS = 50000
        N_EDGES = 25000
        N_ATOM_BASIS = 128
        N_RBF = 20
        N_FILTERS = 128
        LOG2 = 0.6931471805599453

        def ssp(x):
            return jax.nn.softplus(x) - LOG2
        key = jax.random.key(seed)
        ks = jax.random.split(key, 16)
        x = jax.random.normal(ks[0], (N_ATOMS, N_ATOM_BASIS), dtype=jnp.float32)
        f_ij = jax.random.normal(ks[1], (N_EDGES, N_RBF), dtype=jnp.float32)
        rcut_ij = jax.random.uniform(ks[2], (N_EDGES,), dtype=jnp.float32)
        idx_i = jnp.sort(jax.random.randint(ks[3], (N_EDGES,), 0, N_ATOMS))
        idx_j = jax.random.randint(ks[4], (N_EDGES,), 0, N_ATOMS)
        s = lambda fi: 1.0 / np.sqrt(fi)
        W_in2f = jax.random.normal(ks[5], (N_ATOM_BASIS, N_FILTERS), dtype=jnp.float32) * s(N_ATOM_BASIS)
        W_f1 = jax.random.normal(ks[6], (N_RBF, N_FILTERS), dtype=jnp.float32) * s(N_RBF)
        b_f1 = jnp.zeros((N_FILTERS,), dtype=jnp.float32)
        W_f2 = jax.random.normal(ks[7], (N_FILTERS, N_FILTERS), dtype=jnp.float32) * s(N_FILTERS)
        b_f2 = jnp.zeros((N_FILTERS,), dtype=jnp.float32)
        W_o1 = jax.random.normal(ks[8], (N_FILTERS, N_ATOM_BASIS), dtype=jnp.float32) * s(N_FILTERS)
        b_o1 = jnp.zeros((N_ATOM_BASIS,), dtype=jnp.float32)
        W_o2 = jax.random.normal(ks[9], (N_ATOM_BASIS, N_ATOM_BASIS), dtype=jnp.float32) * s(N_ATOM_BASIS)
        b_o2 = jnp.zeros((N_ATOM_BASIS,), dtype=jnp.float32)
        return {'x': x, 'f_ij': f_ij, 'rcut_ij': rcut_ij, 'idx_i': idx_i, 'idx_j': idx_j, 'W_in2f': W_in2f, 'W_f1': W_f1, 'b_f1': b_f1, 'W_f2': W_f2, 'b_f2': b_f2, 'W_o1': W_o1, 'b_o1': b_o1, 'W_o2': W_o2, 'b_o2': b_o2}
    _L0_gnn_all = _L0_gnn_setup()
    _L0_gnn_in = {k: v for k, v in _L0_gnn_all.items() if k in ('W_in2f', 'W_f1', 'b_f1', 'W_f2', 'b_f2', 'W_o1', 'b_o1', 'W_o2', 'b_o2')}
    del _L0_gnn_all
    return {'x': x, 'src': src, 'dst': dst, 'edge_attr_20': edge_attr_20, 'edge_weight': edge_weight, 'L0_gnn_W_in2f': _L0_gnn_in['W_in2f'], 'L0_gnn_W_f1': _L0_gnn_in['W_f1'], 'L0_gnn_b_f1': _L0_gnn_in['b_f1'], 'L0_gnn_W_f2': _L0_gnn_in['W_f2'], 'L0_gnn_b_f2': _L0_gnn_in['b_f2'], 'L0_gnn_W_o1': _L0_gnn_in['W_o1'], 'L0_gnn_b_o1': _L0_gnn_in['b_o1'], 'L0_gnn_W_o2': _L0_gnn_in['W_o2'], 'L0_gnn_b_o2': _L0_gnn_in['b_o2']}

def reference(x, src, dst, edge_attr_20, edge_weight, L0_gnn_W_in2f, L0_gnn_W_f1, L0_gnn_b_f1, L0_gnn_W_f2, L0_gnn_b_f2, L0_gnn_W_o1, L0_gnn_b_o1, L0_gnn_W_o2, L0_gnn_b_o2):
    import jax
    import jax.numpy as jnp

    def _L0_gnn_ref(x, f_ij, rcut_ij, idx_i, idx_j, W_in2f, W_f1, b_f1, W_f2, b_f2, W_o1, b_o1, W_o2, b_o2):
        import jax, jax.numpy as jnp
        import numpy as np
        N_ATOMS = 50000
        N_EDGES = 25000
        N_ATOM_BASIS = 128
        N_RBF = 20
        N_FILTERS = 128
        LOG2 = 0.6931471805599453

        def ssp(x):
            return jax.nn.softplus(x) - LOG2
        h = x @ W_in2f
        Wij = ssp(f_ij @ W_f1 + b_f1) @ W_f2 + b_f2
        Wij = Wij * rcut_ij[:, None]
        x_ij = h[idx_j] * Wij
        agg = jax.ops.segment_sum(x_ij, idx_i, num_segments=h.shape[0])
        out = ssp(agg @ W_o1 + b_o1) @ W_o2 + b_o2
        return out
    x = _layernorm(x + _L0_gnn_ref(x, edge_attr_20, edge_weight, src, dst, L0_gnn_W_in2f, L0_gnn_W_f1, L0_gnn_b_f1, L0_gnn_W_f2, L0_gnn_b_f2, L0_gnn_W_o1, L0_gnn_b_o1, L0_gnn_W_o2, L0_gnn_b_o2), axis=-1)
    return x

_drawn_inputs = setup_inputs


def setup_inputs(seed=0):
    import zlib

    import numpy as np

    out = dict(_drawn_inputs(seed))
    spreads = {'L0_gnn_b_f1': (0.0, 0.727),
     'L0_gnn_b_f2': (0.0, 0.336),
     'L0_gnn_b_o1': (0.0, 0.1),
     'L0_gnn_b_o2': (0.0, 0.1)}
    factors = {}
    for name, (base, spread) in spreads.items():
        noise = np.random.default_rng([zlib.crc32(name.encode()), seed]).standard_normal(out[name].shape)
        drawn = base * np.exp(spread * noise) if base else spread * noise
        out[name] = jnp.asarray(drawn.astype(out[name].dtype))
    for name, factor in factors.items():
        out[name] = (out[name] * factor).astype(out[name].dtype)
    return out
```

```python
import concourse.bass as bass
from concourse import mybir
from contextlib import ExitStack



def gnn_resnorm_kernel(nc, x, dstT, src, srcT, attrT, weightT, W_in2f, W_f1, b_f1, W_f2, b_f2,
                       W_o1, b_o1, W_o2, b_o2, out):
    f32, bf16, i32 = mybir.dt.float32, mybir.dt.bfloat16, mybir.dt.int32
    ALU = mybir.AluOpType
    ACT = mybir.ActivationFunctionType

    N, F = x.shape
    R, E = attrT.shape
    TE, NTILES = dstT.shape
    T = 4
    GE = T * TE
    U = 4
    NI = E // (GE * U)
    LAG = 9
    assert NI * U * GE == E and NTILES * TE == E and F == 128 and LAG < NI - 1
    DUMP = GE

    CN = 12
    Q = CN // 4
    NCH = N // (128 * CN)
    NPP = NCH * CN
    ND = 128 * NPP
    TP, TN = 80, 2
    assert ND + TP * TN == N
    NS = 4
    KN = NCH // NS
    assert NCH == KN * NS + 1

    LOG2 = 0.6931471805599453
    EPS = 1e-5
    EXP_CAP = float(2.0 ** 60)
    assert N + DUMP < (1 << 24)

    agg_dram = nc.dram_tensor("agg_dram", [N + DUMP, F], f32, kind="Internal").ap()
    ZN = 12
    NZ = (N + DUMP) // (128 * ZN)
    ZREST = N + DUMP - NZ * 128 * ZN
    assert ZREST % ZN == 0 and ZREST // ZN <= 128

    def chunked(a):
        return a[0:ND, :].rearrange("(p c) f -> p (c f)", c=NPP)

    def rest(a):
        return a[ND:N, :].rearrange("(p c) f -> p (c f)", c=TN)

    x_ch, agg_ch, out_ch = chunked(x), chunked(agg_dram), chunked(out)

    def wait(engine, semaphore, count):
        if not isinstance(count, int) or count > 0:
            engine.wait_ge(semaphore, count)

    def after(i, j):
        return (i, j + 1) if j + 1 < U else (i + 1, 0)

    ctx = ExitStack()
    with ctx:
        def sb(name, shape, dt=f32):
            return ctx.enter_context(nc.sbuf_tensor(name, shape, dt))

        def sem(name):
            return ctx.enter_context(nc.semaphore(name))

        w_in = sb("w_in", [F, F])
        w_f1 = sb("w_f1", [R, F])
        w_f2 = sb("w_f2", [F, F])
        w_o1 = sb("w_o1", [F, F])
        w_o2 = sb("w_o2", [F, F])
        bf1_col = sb("bf1_col", [F, 1])
        bo1_col = sb("bo1_col", [F, 1])
        b_rows = sb("b_rows", [1, 2, F])
        c_rows = sb("c_rows", [1, 2, F])
        c_parts = sb("c_parts", [1, 2, 3, F], bf16)
        c3 = sb("c3", [3, 2, T, F], bf16)
        ones3 = sb("ones3", [3, 128], bf16)
        neglog2 = sb("neglog2", [128, 1])
        ident = sb("ident", [128, 128])
        zeros = sb("zeros", [128, ZN * F])
        weight = sb("weight", [TE, NTILES])
        src_col = sb("src_col", [TE, NTILES], i32)
        src_f = sb("src_f", [TE, NTILES])
        dump_i = sb("dump_i", [TE, T], i32)
        dump = sb("dump", [TE, T])
        not_after = sb("not_after", [TE, 2 * TE])

        dst_idx = [sb(f"dst_idx{j}", [TE, T], i32) for j in range(U)]
        attr = [sb(f"attr{j}", [R, GE]) for j in range(U)]
        xg = [sb(f"xg{j}", [TE, T, F]) for j in range(U)]
        e1 = sb("e1", [F, GE])
        s1 = [sb(f"s1_{k}", [F, GE]) for k in range(2)]
        xt = [sb(f"xt{k}", [F, GE]) for k in range(2)]
        h = sb("h", [TE, T, F])
        msg = sb("msg", [TE, LAG * U * T * F])
        src_row = [sb(f"src_row{j}", [128, GE], i32) for j in range(U)]
        same = [sb(f"same{k}", [TE, 2, 3 * TE]) for k in range(2)]
        rank = [sb(f"rank{k}", [TE, T]) for k in range(2)]
        dumped = sb("dumped", [TE, T])
        agg_idx = [sb(f"agg_idx{j}", [TE, T], i32) for j in range(U)]
        sums = [sb(f"sums{j}", [TE, T, F]) for j in range(U)]

        xn = [sb(f"xn{s}", [128, CN, F]) for s in range(NS)]
        an = [sb(f"an{s}", [128, CN, F]) for s in range(NS)]
        at = [sb(f"at{k}", [F, 512]) for k in range(2)]
        s2 = [sb(f"s2_{k}", [F, 512]) for k in range(2)]
        e2 = [sb(f"e2_{k}", [F, 512]) for k in range(2)]
        stats = sb("stats", [128, CN, 6])
        dmean = sb("dmean", [128, CN])
        msum = [sb(f"msum{k}", [128, CN]) for k in range(2)]
        m2 = sb("m2", [128, CN])
        var = [sb(f"var{k}", [128, CN]) for k in range(2)]
        rstd0 = [sb(f"rstd0_{k}", [128, CN]) for k in range(2)]
        newton = sb("newton", [128, CN])
        rstd = [sb(f"rstd{k}", [128, CN]) for k in range(2)]
        nmr = [sb(f"nmr{k}", [128, CN]) for k in range(2)]

        bank = [ctx.enter_context(nc.psum_tensor(f"bank{n}", [128, 512], f32)) for n in range(8)]
        z1_ps, xt_ps, h_ps, w_ps, sum_ps = bank[0:5]
        c_ps = bank[7]
        at_ps, z2_ps, y_ps = bank[0:2], bank[2:4], bank[4:6]

        weights_in = sem("weights_in")
        edges_in = sem("edges_in")
        c3_in = sem("c3_in")
        dst_in = [sem(f"dst_in{j}") for j in range(U)]
        src_in = [sem(f"src_in{j}") for j in range(U)]
        attr_in = [sem(f"attr_in{j}") for j in range(U)]
        xg_in = [sem(f"xg_in{j}") for j in range(U)]
        zeroed = sem("zeroed")
        added = sem("added")
        xn_in = [sem(f"xn_in{s}") for s in range(NS)]
        an_in = [sem(f"an_in{s}") for s in range(NS)]
        out_done = [sem(f"out_done{s}") for s in range(NS)]
        zeros_set = sem("zeros_set")
        pool_consts = sem("pool_consts")
        dve_consts = sem("dve_consts")
        colsum_ready = sem("colsum_ready")
        split_step = sem("split_step")
        c_parts_ready = sem("c_parts_ready")
        gather_turns = sem("gather_turns")
        add_turns = sem("add_turns")
        z1_ready = sem("z1_ready")
        e1_ready = sem("e1_ready")
        e1_capped = sem("e1_capped")
        l1_ready = sem("l1_ready")
        s1_ready = sem("s1_ready")
        xtp_ready = sem("xtp_ready")
        xt_ready = sem("xt_ready")
        hp_ready = sem("hp_ready")
        h_ready = sem("h_ready")
        w_ready = sem("w_ready")
        msg_ready = sem("msg_ready")
        same_ready = sem("same_ready")
        dumped_ready = sem("dumped_ready")
        agg_idx_ready = sem("agg_idx_ready")
        sump_ready = sem("sump_ready")
        sums_ready = sem("sums_ready")
        atp_ready = sem("atp_ready")
        at_ready = sem("at_ready")
        z2_ready = sem("z2_ready")
        e2_ready = sem("e2_ready")
        e2_capped = sem("e2_capped")
        l2_ready = sem("l2_ready")
        s2_ready = sem("s2_ready")
        y_ready = sem("y_ready")
        xy_ready = sem("xy_ready")
        stat_step = sem("stat_step")
        var_ready = sem("var_ready")
        lnvar_ready = sem("lnvar_ready")
        rough_ready = sem("rough_ready")
        norm_step = sem("norm_step")
        rstd_ready = sem("rstd_ready")
        norm_ready = sem("norm_ready")
        rows_ready = sem("rows_ready")
        normalise_turns = sem("normalise_turns")

        N_WEIGHTS = 9

        def batch(k, s, q, back):
            n = Q * s + q - back
            turns = n // (Q * NS)
            n -= turns * Q * NS
            return NS * (k + turns) + n // Q, n // Q, n % Q, Q * NS * (k + turns) + n

        def b_slot(s, q):
            return (Q * s + q) % 2

        def real(*at_batch):
            return not isinstance(at_batch[3], int) or at_batch[3] >= 0

        def node_loop(engine, step):
            for s in range(NS):
                for q in range(Q):
                    step(0, s, q)
            with engine.Fori(1, KN) as k:
                for s in range(NS):
                    for q in range(Q):
                        step(k, s, q)
            for q in range(Q):
                step(KN, 0, q)

        LAST = (KN, 0, Q - 1)
        REST = Q * NCH
        RS, RB = 1, REST % 2

        block = ctx.enter_context(nc.Block())

        @block.sync
        def _(sp):
            for j in range(U):
                sp.dma_start(dst_idx[j][:, :], dstT[:, j * T:(j + 1) * T]).then_inc(dst_in[j], 16)
                sp.dma_start(attr[j][:, :], attrT[:, j * GE:(j + 1) * GE]).then_inc(attr_in[j], 16)
            for t, a in ((w_f1, W_f1), (w_in, W_in2f), (w_f2, W_f2), (w_o1, W_o1), (w_o2, W_o2)):
                sp.dma_start(t[:, :], a).then_inc(weights_in, 16)
            sp.dma_start(bf1_col[:, :], b_f1.rearrange("(p a) -> p a", a=1)).then_inc(weights_in, 16)
            sp.dma_start(bo1_col[:, :], b_o1.rearrange("(p a) -> p a", a=1)).then_inc(weights_in, 16)
            sp.dma_start(b_rows[:, 0, :], b_f2.rearrange("(a n) -> a n", a=1)).then_inc(weights_in, 16)
            sp.dma_start(b_rows[:, 1, :], b_o2.rearrange("(a n) -> a n", a=1)).then_inc(weights_in, 16)
            sp.dma_start(weight[:, :], weightT).then_inc(edges_in, 16)
            sp.dma_start(src_col[:, :], srcT).then_inc(edges_in, 16)
            for j in range(U):
                sp.dma_start(src_row[j][:, :], src[j * GE:(j + 1) * GE].partition_broadcast(128)).then_inc(src_in[j], 16)
            sp.wait_ge(c_parts_ready, 1)
            for k in range(2):
                for t in range(T):
                    sp.dma_start(c3[:, k, t, :], c_parts[0:1, k, :, :]).then_inc(c3_in, 16)

            def next_front(i, j):
                sp.wait_ge(xg_in[j], 16 * T * (i + 1))
                sp.dma_start(dst_idx[j][:, :], dstT[:, bass.ds((i + 1) * U * T + j * T, T)]).then_inc(dst_in[j], 16)
                sp.wait_ge(z1_ready, U * i + j + 1)
                sp.dma_start(attr[j][:, :], attrT[:, bass.ds((i + 1) * U * GE + j * GE, GE)]).then_inc(attr_in[j], 16)

            def next_back(i, j):
                sp.wait_ge(same_ready, U * i + j + 1)
                sp.dma_start(src_row[j][:, :],
                             src[bass.ds((i + 1) * U * GE + j * GE, GE)].partition_broadcast(128)).then_inc(src_in[j], 16)

            with sp.Fori(0, LAG) as i:
                for j in range(U):
                    next_front(i, j)
            with sp.Fori(LAG, NI - 1) as i:
                for j in range(U):
                    next_front(i, j)
                    next_back(i - LAG, j)
            with sp.Fori(NI - 1, NI - 1 + LAG) as i:
                for j in range(U):
                    next_back(i - LAG, j)

            def load_x(c, s):
                sp.dma_start(xn[s][:, :, :].rearrange("p c f -> p (c f)"),
                             x_ch[:, bass.ds(c * CN * F, CN * F)]).then_inc(xn_in[s], 16)

            def load_agg(c, s):
                sp.dma_start(an[s][:, :, :].rearrange("p c f -> p (c f)"),
                             agg_ch[:, bass.ds(c * CN * F, CN * F)]).then_inc(an_in[s], 16)

            def store(c, s):
                sp.wait_ge(rows_ready, c + 1)
                sp.dma_start(out_ch[:, bass.ds(c * CN * F, CN * F)],
                             an[s][:, :, :].rearrange("p c f -> p (c f)")).then_inc(out_done[s], 16)

            def reload(c, s, stores):
                load_x(c, s)
                sp.wait_ge(out_done[s], 16 * stores)
                load_agg(c, s)

            for s in range(NS):
                load_x(s, s)
            sp.wait_ge(added, 16 * NTILES)
            for s in range(NS):
                load_agg(s, s)
            store(0, 0)
            for s in range(1, NS):
                store(s, s)
                reload(s - 1 + NS, s - 1, 1)
            with sp.Fori(1, KN - 1) as k:
                store(NS * k, 0)
                reload(NS * k + NS - 1, NS - 1, k)
                for s in range(1, NS):
                    store(NS * k + s, s)
                    reload(NS * (k + 1) + s - 1, s - 1, k + 1)
            k = KN - 1
            store(NS * k, 0)
            reload(NS * k + NS - 1, NS - 1, k)
            store(NS * k + 1, 1)
            reload(NCH - 1, 0, k + 1)
            store(NS * k + 2, 2)
            sp.dma_start(xn[RS][0:TP, 0:TN, :].rearrange("p c f -> p (c f)"), rest(x)).then_inc(xn_in[RS], 16)
            sp.wait_ge(out_done[RS], 16 * KN)
            sp.dma_start(an[RS][0:TP, 0:TN, :].rearrange("p c f -> p (c f)"), rest(agg_dram)).then_inc(an_in[RS], 16)
            store(NS * k + 3, 3)
            store(NCH - 1, 0)
            sp.wait_ge(rows_ready, NCH + 1)
            sp.dma_start(rest(out), an[RS][0:TP, 0:TN, :].rearrange("p c f -> p (c f)")).then_inc(out_done[RS], 16)
            for s in range(NS):
                sp.wait_ge(out_done[s], 16 * (KN + (s in (0, RS))))

        @block.gpsimd
        def _(pool):
            def gather(i, j, tiles):
                for t in tiles:
                    pool.indirect_dma_start(
                        out=xg[j][:, t, :], out_offset=None, in_=x,
                        in_offset=bass.IndirectOffsetOnAxis(ap=dst_idx[j][:, t:t + 1], axis=0),
                    ).then_inc(xg_in[j], 16)

            def ready_to_gather(i, j):
                pool.wait_ge(dst_in[j], 16 * (i + 1))
                wait(pool, xtp_ready, U * (i - 1) + j + 1)
                pool.sem_inc(gather_turns, 1)

            def add_pair(i, j, pair):
                wait(pool, added, 16 * (T * (U * i + j) + 2 * pair))
                pool.wait_ge(agg_idx_ready, U * i + j + 1)
                pool.wait_ge(sums_ready, U * i + j + 1)
                pool.sem_inc(add_turns, 1)
                for t in (2 * pair, 2 * pair + 1):
                    pool.indirect_dma_start(
                        out=agg_dram, in_=sums[j][:, t, :], in_offset=None,
                        out_offset=bass.IndirectOffsetOnAxis(ap=agg_idx[j][:, t:t + 1], axis=0),
                        compute_op=ALU.add,
                    ).then_inc(added, 16)

            nc.gpsimd.memset(ident[:, :], 0.0).then_inc(pool_consts, 1)
            nc.gpsimd.memset(not_after[:, :], 1.0).then_inc(pool_consts, 1)
            ready_to_gather(0, 0)
            gather(0, 0, range(T))
            pool.wait_ge(pool_consts, 2)
            pool.affine_select(out=ident[:, :], in_=ident[:, :], compare_op=ALU.not_equal, fill=1.0,
                               base=0, pattern=[[-1, 128]], channel_multiplier=1).then_inc(pool_consts, 1)
            pool.affine_select(out=not_after[:, :], in_=not_after[:, :], compare_op=ALU.is_ge, fill=0.0,
                               base=TE, pattern=[[-1, 2 * TE]], channel_multiplier=1).then_inc(pool_consts, 1)
            pool.iota(dump_i[:, :], pattern=[[TE, T]], base=N, channel_multiplier=1).then_inc(pool_consts, 1)
            for j in range(1, U):
                ready_to_gather(0, j)
                gather(0, j, range(T))
            with pool.Fori(1, LAG + 1) as i:
                for j in range(U):
                    ready_to_gather(i, j)
                    gather(i, j, range(T))
            pool.wait_ge(zeroed, 16 * (NZ + 1))
            pool.sem_inc(add_turns, 1)

            def gather_and_add(i, j):
                for pair in range(2):
                    if pair == 0:
                        ready_to_gather(i + 1, j)
                    gather(i + 1, j, (2 * pair, 2 * pair + 1))
                    add_pair(i - LAG, j, pair)

            for j in range(U):
                gather_and_add(LAG, j)
            with pool.Fori(LAG + 1, NI - 1) as i:
                for j in range(U):
                    gather_and_add(i, j)
            with pool.Fori(NI - 1, NI + LAG) as i:
                for j in range(U):
                    for pair in range(2):
                        add_pair(i - LAG, j, pair)

            def normalise(c, s, P=128, C=CN):
                pool.wait_ge(norm_ready, c + 1)
                pool.sem_inc(normalise_turns, 1)
                for r in range(C):
                    last = nc.gpsimd.tensor_scalar(an[s][0:P, r, :], xn[s][0:P, r, :], rstd[s % 2][0:P, r:r + 1],
                                                   nmr[s % 2][0:P, r:r + 1], ALU.mult, ALU.add)
                last.then_inc(rows_ready, 1)

            with pool.Fori(0, KN) as k:
                for s in range(NS):
                    normalise(NS * k + s, s)
            normalise(NCH - 1, 0)
            normalise(NCH, RS, TP, TN)

        @block.tensor
        def _(pe):
            pe.wait_ge(weights_in, 16 * N_WEIGHTS)
            pe.wait_ge(dve_consts, 1)
            nc.tensor.matmul(c_ps[0:1, 0:F], neglog2[:, :], w_f2[:, :], start=True, stop=True)
            nc.tensor.matmul(c_ps[0:1, F:2 * F], neglog2[:, :], w_o2[:, :], start=True, stop=True).then_inc(colsum_ready, 1)
            pe.wait_ge(pool_consts, 5)
            pe.wait_ge(c3_in, 16 * 2 * T)

            def filter_in(i, j):
                n = U * i + j
                pe.wait_ge(attr_in[j], 16 * (i + 1))
                wait(pe, s1_ready, n)
                nc.tensor.matmul(z1_ps[:, 0:GE], w_f1[:, :], attr[j][:, :], start=True, stop=True).then_inc(z1_ready, 1)
                pe.wait_ge(xg_in[j], 16 * T * (i + 1))
                wait(pe, xt_ready, n)
                for t in range(T):
                    last = nc.tensor.transpose(xt_ps[:, t * TE:(t + 1) * TE], xg[j][:, t, :], ident[0:TE, 0:TE])
                last.then_inc(xtp_ready, 1)

            def message(i, j):
                n = U * i + j
                pe.wait_ge(xt_ready, n + 1)
                wait(pe, h_ready, n)
                for t in range(T):
                    last = nc.tensor.matmul(h_ps[0:TE, t * F:(t + 1) * F], xt[j % 2][:, t * TE:(t + 1) * TE],
                                            w_in[:, :], start=True, stop=True)
                last.then_inc(hp_ready, 1)
                wait(pe, msg_ready, n)
                pe.wait_ge(s1_ready, n + 1)
                nc.tensor.matmul(w_ps[0:TE, :], ones3[:, 0:TE], c3[:, 0, :, :].rearrange("p t f -> p (t f)"),
                                 start=True, stop=False, skip_group_check=True)
                for t in range(T):
                    last = nc.tensor.matmul(w_ps[0:TE, t * F:(t + 1) * F], s1[j % 2][:, t * TE:(t + 1) * TE], w_f2[:, :],
                                            start=False, stop=(t == T - 1), skip_group_check=True)
                last.then_inc(w_ready, 1)

            def sum_pairs(i, j):
                n = U * i + j
                pe.wait_ge(same_ready, n + 1)
                wait(pe, sums_ready, n)
                ring = (i % LAG) * (U * T * F) + j * T * F
                for pair in range(2):
                    t0, t1 = 2 * pair, 2 * pair + 1
                    m0, m1 = (msg[:, bass.ds(ring + t * F, F)] for t in (t0, t1))
                    eq = same[j % 2][:, pair, :]
                    nc.tensor.matmul(sum_ps[0:TE, t0 * F:(t0 + 1) * F], eq[:, 0:TE], m0, start=True, stop=False)
                    nc.tensor.matmul(sum_ps[0:TE, t0 * F:(t0 + 1) * F], eq[:, TE:2 * TE], m1, start=False, stop=True)
                    last = nc.tensor.matmul(sum_ps[0:TE, t1 * F:(t1 + 1) * F], eq[:, 2 * TE:3 * TE], m1,
                                            start=True, stop=True)
                last.then_inc(sump_ready, 1)

            filter_in(0, 0)
            for j in range(U):
                filter_in(*after(0, j))
                message(0, j)
            with pe.Fori(1, LAG) as i:
                for j in range(U):
                    filter_in(*after(i, j))
                    message(i, j)

            def both(i, j):
                sum_pairs(i - LAG, j)
                filter_in(*after(i, j))
                message(i, j)

            for j in range(U):
                both(LAG, j)
            with pe.Fori(LAG + 1, NI - 1) as i:
                for j in range(U):
                    both(i, j)
            for j in range(U):
                sum_pairs(NI - 1 - LAG, j)
                if j + 1 < U:
                    filter_in(NI - 1, j + 1)
                message(NI - 1, j)
            with pe.Fori(NI, NI + LAG) as i:
                for j in range(U):
                    sum_pairs(i - LAG, j)

            pe.wait_ge(sums_ready, NI * U)

            def transpose_agg(c, s, q, b, k, P=128, tiles=4):
                pe.wait_ge(an_in[s], 16 * (k + 1))
                wait(pe, at_ready, b - 1)
                for t in range(tiles):
                    last = nc.tensor.transpose(at_ps[b_slot(s, q)][:, t * P:(t + 1) * P], an[s][0:P, 4 * q + t, :],
                                               ident[0:P, 0:P])
                last.then_inc(atp_ready, 1)

            def hidden(c, s, q, b, W=512):
                pe.wait_ge(at_ready, b + 1)
                wait(pe, s2_ready, b - 1)
                p = b_slot(s, q)
                nc.tensor.matmul(z2_ps[p][:, 0:W], w_o1[:, :], at[p][:, 0:W], start=True, stop=True).then_inc(z2_ready, 1)

            def update(c, s, q, b, P=128, tiles=4):
                pe.wait_ge(s2_ready, b + 1)
                wait(pe, xy_ready, b - 1)
                p = b_slot(s, q)
                nc.tensor.matmul(y_ps[p][0:P, 0:tiles * F], ones3[:, 0:P], c3[:, 1, 0:tiles, :].rearrange("p t f -> p (t f)"),
                                 start=True, stop=False, skip_group_check=True)
                for t in range(tiles):
                    last = nc.tensor.matmul(y_ps[p][0:P, t * F:(t + 1) * F], s2[p][:, t * P:(t + 1) * P], w_o2[:, :],
                                            start=False, stop=(t == tiles - 1), skip_group_check=True)
                last.then_inc(y_ready, 1)

            def step(k, s, q):
                transpose_agg(*batch(k, s, q, 0), k)
                for stage, back in ((hidden, 1), (update, 3)):
                    if real(*batch(k, s, q, back)):
                        stage(*batch(k, s, q, back))

            node_loop(pe, step)
            the_rest = (NCH, RS, 0, REST)
            transpose_agg(*the_rest, KN, TP, TN)
            hidden(*batch(*LAST, 0))
            update(*batch(*LAST, 2))
            hidden(*the_rest, TP * TN)
            update(*batch(*LAST, 1))
            update(*batch(*LAST, 0))
            update(*the_rest, TP, TN)

        @block.scalar
        def _(act):
            act.preload_act_table_set("natural_log_exp_and_others")

            act.wait_ge(zeros_set, 1)
            z_ch = agg_dram[0:NZ * 128 * ZN, :].rearrange("(n p c) f -> n p (c f)", p=128, c=ZN)
            for n in range(NZ):
                act.dma_start(z_ch[n, :, :], zeros[:, :]).then_inc(zeroed, 16)
            act.dma_start(agg_dram[NZ * 128 * ZN:N + DUMP, :].rearrange("(p c) f -> p (c f)", c=ZN),
                          zeros[0:ZREST // ZN, :]).then_inc(zeroed, 16)
            act.wait_ge(weights_in, 16 * N_WEIGHTS)

            def exp1(i, j):
                n = U * i + j
                act.wait_ge(z1_ready, n + 1)
                wait(act, s1_ready, n)
                nc.scalar.activation(e1[:, :], z1_ps[:, 0:GE], ACT.Exp, bias=bf1_col[:, :]).then_inc(e1_ready, 1)

            def copy_xt(i, j):
                n = U * i + j
                act.wait_ge(xtp_ready, n + 1)
                wait(act, hp_ready, n - 1)
                nc.scalar.activation(xt[j % 2][:, :], xt_ps[:, 0:GE], ACT.Copy).then_inc(xt_ready, 1)

            def copy_h(i, j):
                n = U * i + j
                act.wait_ge(hp_ready, n + 1)
                wait(act, msg_ready, n)
                nc.scalar.activation(h[:, :, :].rearrange("p t f -> p (t f)"), h_ps[0:TE, :],
                                     ACT.Copy).then_inc(h_ready, 1)

            def ln1(i, j):
                act.wait_ge(e1_capped, U * i + j + 1)
                nc.scalar.activation(e1[:, :], e1[:, :], ACT.Ln, bias=1.0).then_inc(l1_ready, 1)

            def copy_sums(i, j):
                n = U * i + j
                act.wait_ge(sump_ready, n + 1)
                wait(act, added, 16 * T * (n - U + 1))
                nc.scalar.activation(sums[j][:, :, :].rearrange("p t f -> p (t f)"), sum_ps[0:TE, :],
                                     ACT.Copy).then_inc(sums_ready, 1)

            def front(i, j):
                exp1(*after(i, j))
                copy_h(i, j)
                ln1(*after(i, j))
                copy_xt(*after(i, j))

            def both(i, j):
                copy_sums(i - LAG, j)
                front(i, j)

            exp1(0, 0)
            copy_xt(0, 0)
            ln1(0, 0)
            for j in range(U):
                front(0, j)
            with act.Fori(1, LAG) as i:
                for j in range(U):
                    front(i, j)
            for j in range(U):
                both(LAG, j)
            with act.Fori(LAG + 1, NI - 1) as i:
                for j in range(U):
                    both(i, j)
            for j in range(U):
                copy_sums(NI - 1 - LAG, j)
                if j + 1 < U:
                    front(NI - 1, j)
                else:
                    copy_h(NI - 1, j)
            with act.Fori(NI, NI + LAG) as i:
                for j in range(U):
                    copy_sums(i - LAG, j)

            def copy_at(c, s, q, b, W=512):
                p = b_slot(s, q)
                act.wait_ge(atp_ready, b + 1)
                wait(act, z2_ready, b - 1)
                nc.scalar.activation(at[p][:, 0:W], at_ps[p][:, 0:W], ACT.Copy).then_inc(at_ready, 1)

            def exp2(c, s, q, b, W=512):
                p = b_slot(s, q)
                act.wait_ge(z2_ready, b + 1)
                wait(act, s2_ready, b - 1)
                nc.scalar.activation(e2[p][:, 0:W], z2_ps[p][:, 0:W], ACT.Exp, bias=bo1_col[:, :]).then_inc(e2_ready, 1)

            def ln2(c, s, q, b, W=512):
                p = b_slot(s, q)
                act.wait_ge(e2_capped, b + 1)
                nc.scalar.activation(e2[p][:, 0:W], e2[p][:, 0:W], ACT.Ln, bias=1.0).then_inc(l2_ready, 1)

            def rough_rstd(c, s, P=128, C=CN):
                r0 = rstd0[s % 2][0:P, 0:C]
                act.wait_ge(var_ready, c + 1)
                nc.scalar.activation(r0, var[s % 2][0:P, 0:C], ACT.Ln).then_inc(lnvar_ready, 1)
                act.wait_ge(lnvar_ready, c + 1)
                nc.scalar.activation(r0, r0, ACT.Exp, scale=-0.5).then_inc(rough_ready, 1)

            def step(k, s, q):
                copy_at(*batch(k, s, q, 0))
                for stage, back in ((exp2, 1), (ln2, 2)):
                    if real(*batch(k, s, q, back)):
                        stage(*batch(k, s, q, back))
                c, cs, cq, b = batch(k, s, q, 4)
                if cq == Q - 1 and real(c, cs, cq, b):
                    rough_rstd(c, cs)

            node_loop(act, step)
            the_rest = (NCH, RS, 0, REST)
            copy_at(*the_rest, TP * TN)
            exp2(*batch(*LAST, 0))
            ln2(*batch(*LAST, 1))
            rough_rstd(NCH - 2, NS - 1)
            exp2(*the_rest, TP * TN)
            ln2(*batch(*LAST, 0))
            ln2(*the_rest, TP * TN)
            rough_rstd(NCH - 1, 0)
            rough_rstd(NCH, RS, TP, TN)

        @block.vector
        def _(dve):
            nc.vector.memset(zeros[:, :], 0.0).then_inc(zeros_set, 1)
            nc.vector.memset(neglog2[:, :], -LOG2)
            nc.vector.memset(ones3[:, :], 1.0).then_inc(dve_consts, 1)
            dve.wait_ge(weights_in, 16 * N_WEIGHTS)
            dve.wait_ge(colsum_ready, 1)
            nc.vector.tensor_tensor(c_rows[:, :, :], c_ps[0:1, 0:2 * F].rearrange("p (k f) -> p k f", k=2),
                                    b_rows[:, :, :], ALU.add).then_inc(split_step, 1)
            for part in range(3):
                dve.wait_ge(split_step, 1 + 2 * part)
                nc.vector.tensor_copy(c_parts[:, :, part, :], c_rows[:, :, :]).then_inc(
                    c_parts_ready if part == 2 else split_step, 1)
                if part < 2:
                    dve.wait_ge(split_step, 2 + 2 * part)
                    nc.vector.tensor_tensor(c_rows[:, :, :], c_rows[:, :, :], c_parts[:, :, part, :],
                                            ALU.subtract).then_inc(split_step, 1)
            dve.wait_ge(edges_in, 16 * 2)
            nc.vector.tensor_copy(src_f[:, :], src_col[:, :]).then_inc(dve_consts, 1)
            dve.wait_ge(pool_consts, 5)
            nc.vector.tensor_copy(dump[:, :], dump_i[:, :]).then_inc(dve_consts, 1)
            dve.wait_ge(dve_consts, 3)

            def cap1(i, j):
                dve.wait_ge(e1_ready, U * i + j + 1)
                nc.vector.tensor_scalar(e1[:, :], e1[:, :], EXP_CAP, None, ALU.min).then_inc(e1_capped, 1)

            def softplus1(i, j):
                n = U * i + j
                dve.wait_ge(l1_ready, n + 1)
                wait(dve, w_ready, n - 1)
                nc.vector.scalar_tensor_tensor(s1[j % 2][:, :], z1_ps[:, 0:GE], bf1_col[:, :], e1[:, :],
                                               ALU.add, ALU.max).then_inc(s1_ready, 1)

            def message(i, j):
                dve.wait_ge(h_ready, U * i + j + 1)
                dve.wait_ge(w_ready, U * i + j + 1)
                ring = (i % LAG) * (U * T * F) + j * T * F
                for t in range(T):
                    last = nc.vector.scalar_tensor_tensor(
                        msg[:, bass.ds(ring + t * F, F)], w_ps[0:TE, t * F:(t + 1) * F],
                        weight[:, bass.ds(U * T * i + T * j + t, 1)], h[:, t, :], ALU.mult, ALU.mult)
                last.then_inc(msg_ready, 1)

            def mark(i, j):
                n = U * i + j
                dve.wait_ge(src_in[j], 16 * (i + 1))
                wait(dve, sump_ready, n - 1)
                for pair in range(2):
                    for t, cols in ((0, TE), (1, 2 * TE)):
                        tile = 2 * pair + t
                        last = nc.vector.scalar_tensor_tensor(
                            same[j % 2][:, pair, TE * t:TE * t + cols],
                            src_row[j][0:TE, 2 * TE * pair:2 * TE * pair + cols],
                            src_f[:, bass.ds(U * T * i + T * j + tile, 1)],
                            not_after[:, 2 * TE - cols:2 * TE], ALU.is_equal, ALU.mult,
                            accum_out=rank[j % 2][:, tile:tile + 1])
                last.then_inc(same_ready, 1)

            def index(i, j):
                n = U * i + j
                dve.wait_ge(same_ready, n + 1)
                nc.vector.scalar_tensor_tensor(dumped[:, :], rank[j % 2][:, :], 1.5, dump[:, :],
                                               ALU.is_gt, ALU.mult).then_inc(dumped_ready, 1)
                dve.wait_ge(dumped_ready, n + 1)
                wait(dve, added, 16 * T * (n - U + 1))
                nc.vector.tensor_tensor(agg_idx[j][:, :], dumped[:, :], src_f[:, bass.ds(U * T * i + T * j, T)],
                                        ALU.max).then_inc(agg_idx_ready, 1)

            def front(i, j):
                cap1(*after(i, j))
                message(i, j)
                softplus1(*after(i, j))

            def both(i, j):
                mark(i - LAG, j)
                cap1(*after(i, j))
                message(i, j)
                index(i - LAG, j)
                softplus1(*after(i, j))

            cap1(0, 0)
            softplus1(0, 0)
            for j in range(U):
                front(0, j)
            with dve.Fori(1, LAG) as i:
                for j in range(U):
                    front(i, j)
            for j in range(U):
                both(LAG, j)
            with dve.Fori(LAG + 1, NI - 1) as i:
                for j in range(U):
                    both(i, j)
            for j in range(U):
                mark(NI - 1 - LAG, j)
                if j + 1 < U:
                    cap1(NI - 1, j + 1)
                message(NI - 1, j)
                index(NI - 1 - LAG, j)
                if j + 1 < U:
                    softplus1(NI - 1, j + 1)
            with dve.Fori(NI, NI + LAG) as i:
                for j in range(U):
                    mark(i - LAG, j)
                    index(i - LAG, j)

            def cap2(c, s, q, b, W=512):
                p = b_slot(s, q)
                dve.wait_ge(e2_ready, b + 1)
                nc.vector.tensor_scalar(e2[p][:, 0:W], e2[p][:, 0:W], EXP_CAP, None, ALU.min).then_inc(e2_capped, 1)

            def softplus2(c, s, q, b, W=512):
                p = b_slot(s, q)
                dve.wait_ge(l2_ready, b + 1)
                wait(dve, y_ready, b - 1)
                nc.vector.scalar_tensor_tensor(s2[p][:, 0:W], z2_ps[p][:, 0:W], bo1_col[:, :], e2[p][:, 0:W],
                                               ALU.add, ALU.max).then_inc(s2_ready, 1)

            def residual(c, s, q, b, loads, P=128, tiles=4):
                rows = xn[s][0:P, 4 * q:4 * q + tiles, :]
                if q == 0:
                    dve.wait_ge(xn_in[s], 16 * loads)
                dve.wait_ge(y_ready, b + 1)
                nc.vector.tensor_tensor(rows, y_ps[b_slot(s, q)][0:P, 0:tiles * F].rearrange("p (t f) -> p t f", t=tiles),
                                        rows, ALU.add).then_inc(xy_ready, 1)
                dve.wait_ge(xy_ready, b + 1)
                for r in range(4 * q, 4 * q + tiles):
                    last = nc.vector.bn_stats(stats[0:P, r, :], xn[s][0:P, r, :])
                return last

            def moments(c, s, P=128, C=CN):
                mean_e, m2_e, mean_o, m2_o = (stats[0:P, 0:C, m] for m in (1, 2, 4, 5))
                dve.wait_ge(stat_step, 4 * c + 1)
                nc.vector.tensor_tensor(dmean[0:P, 0:C], mean_e, mean_o, ALU.subtract)
                nc.vector.tensor_tensor(msum[s % 2][0:P, 0:C], mean_e, mean_o, ALU.add)
                nc.vector.tensor_tensor(m2[0:P, 0:C], m2_e, m2_o, ALU.add).then_inc(stat_step, 1)
                dve.wait_ge(stat_step, 4 * c + 2)
                nc.vector.tensor_tensor(dmean[0:P, 0:C], dmean[0:P, 0:C], dmean[0:P, 0:C], ALU.mult).then_inc(stat_step, 1)
                dve.wait_ge(stat_step, 4 * c + 3)
                nc.vector.scalar_tensor_tensor(m2[0:P, 0:C], dmean[0:P, 0:C], F / 4.0, m2[0:P, 0:C],
                                               ALU.mult, ALU.add).then_inc(stat_step, 1)
                dve.wait_ge(stat_step, 4 * c + 4)
                wait(dve, rstd_ready, c - 1)
                nc.vector.tensor_scalar(var[s % 2][0:P, 0:C], m2[0:P, 0:C], 1.0 / F, EPS,
                                        ALU.mult, ALU.add).then_inc(var_ready, 1)

            def refine(c, s, P=128, C=CN):
                r0, r, v = (a[s % 2][0:P, 0:C] for a in (rstd0, rstd, var))
                dve.wait_ge(rough_ready, c + 1)
                nc.vector.tensor_tensor(newton[0:P, 0:C], r0, r0, ALU.mult).then_inc(norm_step, 1)
                dve.wait_ge(norm_step, 2 * c + 1)
                nc.vector.scalar_tensor_tensor(newton[0:P, 0:C], newton[0:P, 0:C], -0.5, v,
                                               ALU.mult, ALU.mult).then_inc(norm_step, 1)
                dve.wait_ge(norm_step, 2 * c + 2)
                wait(dve, rows_ready, c - 1)
                nc.vector.scalar_tensor_tensor(r, newton[0:P, 0:C], 1.5, r0, ALU.add, ALU.mult).then_inc(rstd_ready, 1)
                dve.wait_ge(rstd_ready, c + 1)
                nc.vector.scalar_tensor_tensor(nmr[s % 2][0:P, 0:C], msum[s % 2][0:P, 0:C], -0.5, r,
                                               ALU.mult, ALU.mult).then_inc(norm_ready, 1)

            def sum_up(k, s, q):
                c, cs, cq, b = batch(k, s, q, 3)
                if real(c, cs, cq, b):
                    turn = k if Q * s + q >= 3 else k - 1
                    last = residual(c, cs, cq, b, turn + 1)
                    if cq == Q - 1:
                        last.then_inc(stat_step, 1)
                        moments(c, cs)
                c, cs, cq, b = batch(k, s, q, 5)
                if cq == Q - 1 and real(c, cs, cq, b):
                    refine(c, cs)

            def step(k, s, q):
                for stage, back in ((cap2, 1), (softplus2, 2)):
                    if real(*batch(k, s, q, back)):
                        stage(*batch(k, s, q, back))
                sum_up(k, s, q)

            node_loop(dve, step)
            the_rest = (NCH, RS, 0, REST)
            cap2(*batch(*LAST, 0))
            softplus2(*batch(*LAST, 1))
            residual(*batch(*LAST, 2), KN + 1)
            cap2(*the_rest, TP * TN)
            softplus2(*batch(*LAST, 0))
            residual(*batch(*LAST, 1), KN + 1)
            refine(NCH - 2, NS - 1)
            softplus2(*the_rest, TP * TN)
            residual(*batch(*LAST, 0), KN + 1).then_inc(stat_step, 1)
            moments(NCH - 1, 0)
            residual(*the_rest, KN + 1, TP, TN).then_inc(stat_step, 1)
            moments(NCH, RS, TP, TN)
            refine(NCH - 1, 0)
            refine(NCH, RS, TP, TN)


def kernel(x, src, dst, edge_attr_20, edge_weight, L0_gnn_W_in2f, L0_gnn_W_f1, L0_gnn_b_f1, L0_gnn_W_f2,
           L0_gnn_b_f2, L0_gnn_W_o1, L0_gnn_b_o1, L0_gnn_W_o2, L0_gnn_b_o2):
    import numpy as _np
    import concourse.bacc as _bacc
    from concourse import mybir as _mybir
    from concourse.bass_utils import run_bass_kernel_spmd as _run

    TILE = 125

    def tiled(a):
        return _np.ascontiguousarray(_np.asarray(a).reshape(-1, TILE).T)

    arrays = {
        "x": x, "dstT": tiled(dst), "src": src, "srcT": tiled(src),
        "attrT": _np.asarray(edge_attr_20).T, "weightT": tiled(edge_weight),
        "W_in2f": L0_gnn_W_in2f, "W_f1": L0_gnn_W_f1, "b_f1": L0_gnn_b_f1, "W_f2": L0_gnn_W_f2,
        "b_f2": L0_gnn_b_f2, "W_o1": L0_gnn_W_o1, "b_o1": L0_gnn_b_o1, "W_o2": L0_gnn_W_o2, "b_o2": L0_gnn_b_o2,
    }
    arrays = {k: _np.ascontiguousarray(v) for k, v in arrays.items()}
    nc = _bacc.Bacc("TRN2", target_bir_lowering=False, num_devices=1)
    args = [nc.dram_tensor(k, a.shape, _mybir.dt.from_np(a.dtype), kind="ExternalInput").ap()
            for k, a in arrays.items()]
    out = nc.dram_tensor("out", arrays["x"].shape, _mybir.dt.float32, kind="ExternalOutput").ap()
    gnn_resnorm_kernel(nc, *args, out)
    r = _run(nc, [arrays], core_ids=[0])
    return r.results[0]["out"]
```

```python
import concourse.bass as bass
from concourse import mybir
from contextlib import ExitStack



def gnn_resnorm_kernel(nc, x, dstT, src, srcT, attrT, weightT, W_in2f, W_f1, b_f1, W_f2, b_f2,
                       W_o1, b_o1, W_o2, b_o2, out):
    f32, bf16, i32 = mybir.dt.float32, mybir.dt.bfloat16, mybir.dt.int32
    ALU = mybir.AluOpType
    ACT = mybir.ActivationFunctionType

    N, F = x.shape
    R, E = attrT.shape
    TE, NTILES = dstT.shape
    T = 4
    GE = T * TE
    U = 4
    NI = E // (GE * U)
    LAG = 9
    assert NI * U * GE == E and NTILES * TE == E and F == 128 and LAG < NI - 1
    RING = LAG + 1
    DUMP = GE

    CN = 12
    Q = CN // 4
    NCH = N // (128 * CN)
    NPP = NCH * CN
    ND = 128 * NPP
    TP, TN = 80, 2
    assert ND + TP * TN == N
    NS = 4
    KN = NCH // NS
    assert NCH == KN * NS + 1

    LOG2 = 0.6931471805599453
    EPS = 1e-5
    assert N + DUMP < (1 << 24)

    agg_dram = nc.dram_tensor("agg_dram", [N + DUMP, F], f32, kind="Internal").ap()
    ZN = 12
    NZ = (N + DUMP) // (128 * ZN)
    ZREST = N + DUMP - NZ * 128 * ZN
    assert ZREST % ZN == 0 and ZREST // ZN <= 128

    def chunked(a):
        return a[0:ND, :].rearrange("(p c) f -> p (c f)", c=NPP)

    def rest(a):
        return a[ND:N, :].rearrange("(p c) f -> p (c f)", c=TN)

    x_ch, agg_ch, out_ch = chunked(x), chunked(agg_dram), chunked(out)

    def wait(engine, semaphore, count):
        if not isinstance(count, int) or count > 0:
            engine.wait_ge(semaphore, count)

    def after(i, j):
        return (i, j + 1) if j + 1 < U else (i + 1, 0)

    ctx = ExitStack()
    with ctx:
        def sb(name, shape, dt=f32):
            return ctx.enter_context(nc.sbuf_tensor(name, shape, dt))

        def sem(name):
            return ctx.enter_context(nc.semaphore(name))

        w_in = sb("w_in", [F, F])
        w_f1 = sb("w_f1", [R, F])
        w_f2 = sb("w_f2", [F, F])
        w_o1 = sb("w_o1", [F, F])
        w_o2 = sb("w_o2", [F, F])
        bf1_col = sb("bf1_col", [F, 1])
        bo1_col = sb("bo1_col", [F, 1])
        b_rows = sb("b_rows", [1, 2, F])
        c_rows = sb("c_rows", [1, 2, F])
        c_parts = sb("c_parts", [1, 2, 3, F], bf16)
        c3 = sb("c3", [3, 2, T, F], bf16)
        ones3 = sb("ones3", [3, 128], bf16)
        neg_bf1, neg_bo1 = sb("neg_bf1", [F, 1]), sb("neg_bo1", [F, 1])
        left_f1, left_o1 = sb("left_f1", [F, 1]), sb("left_o1", [F, 1])
        ident = sb("ident", [128, 128])
        zeros = sb("zeros", [128, ZN * F])
        weight = sb("weight", [TE, NTILES])
        src_col = sb("src_col", [TE, NTILES], i32)
        src_f = sb("src_f", [TE, NTILES])
        dump_i = sb("dump_i", [TE, T], i32)
        dump = sb("dump", [TE, T])
        not_after = sb("not_after", [TE, 2 * TE])

        dst_idx = [sb(f"dst_idx{j}", [TE, T], i32) for j in range(U)]
        attr = [sb(f"attr{j}", [R, GE]) for j in range(U)]
        xg = [sb(f"xg{j}", [TE, T, F]) for j in range(U)]
        e1 = sb("e1", [F, GE])
        s1 = [sb(f"s1_{k}", [F, GE]) for k in range(2)]
        xt = [sb(f"xt{k}", [F, GE]) for k in range(2)]
        h = sb("h", [TE, T, F])
        msg = sb("msg", [128, RING * U * T * F])
        src_row = [sb(f"src_row{j}", [128, GE], i32) for j in range(U)]
        same = [sb(f"same{k}", [TE, 2, 3 * TE]) for k in range(2)]
        rank = [sb(f"rank{k}", [TE, T]) for k in range(2)]
        dumped = sb("dumped", [TE, T])
        agg_idx = [sb(f"agg_idx{j}", [TE, T], i32) for j in range(U)]
        sums = [sb(f"sums{j}", [TE, T, F]) for j in range(U)]

        xn = [sb(f"xn{s}", [128, CN, F]) for s in range(NS)]
        an, rows_out = ([msg[:, n * CN * F:(n + 1) * CN * F].rearrange("p (c f) -> p c f", c=CN)
                         for n in range(a, a + NS)] for a in (0, NS))
        at = [sb(f"at{k}", [F, 512]) for k in range(2)]
        s2 = [sb(f"s2_{k}", [F, 512]) for k in range(2)]
        e2 = [sb(f"e2_{k}", [F, 512]) for k in range(2)]
        stats = sb("stats", [128, CN, 6])
        dmean = sb("dmean", [128, CN])
        msum = [sb(f"msum{k}", [128, CN]) for k in range(2)]
        m2 = sb("m2", [128, CN])
        var = [sb(f"var{k}", [128, CN]) for k in range(2)]
        rstd0 = [sb(f"rstd0_{k}", [128, CN]) for k in range(2)]
        newton = sb("newton", [128, CN])
        rstd = [sb(f"rstd{k}", [128, CN]) for k in range(2)]
        nmr = [sb(f"nmr{k}", [128, CN]) for k in range(2)]

        bank = [ctx.enter_context(nc.psum_tensor(f"bank{n}", [128, 512], f32)) for n in range(8)]
        z1_ps, xt_ps, h_ps, w_ps, sum_ps = bank[0:5]
        c_ps = bank[7]
        at_ps, z2_ps, y_ps = bank[0:2], bank[2:4], bank[4:6]

        weights_in = sem("weights_in")
        edges_in = sem("edges_in")
        c3_in = sem("c3_in")
        dst_in = [sem(f"dst_in{j}") for j in range(U)]
        src_in = [sem(f"src_in{j}") for j in range(U)]
        attr_in = [sem(f"attr_in{j}") for j in range(U)]
        xg_in = [sem(f"xg_in{j}") for j in range(U)]
        zeroed = sem("zeroed")
        added = sem("added")
        xn_in = [sem(f"xn_in{s}") for s in range(NS)]
        an_in = [sem(f"an_in{s}") for s in range(NS)]
        out_done = [sem(f"out_done{s}") for s in range(NS)]
        zeros_set = sem("zeros_set")
        pool_consts = sem("pool_consts")
        dve_consts = sem("dve_consts")
        left_ready = sem("left_ready")
        split_step = sem("split_step")
        c_parts_ready = sem("c_parts_ready")
        gather_turns = sem("gather_turns")
        add_turns = sem("add_turns")
        z1_ready = sem("z1_ready")
        abs1_ready = sem("abs1_ready")
        e1_ready = sem("e1_ready")
        l1_ready = sem("l1_ready")
        s1_ready = sem("s1_ready")
        xtp_ready = sem("xtp_ready")
        xt_ready = sem("xt_ready")
        hp_ready = sem("hp_ready")
        h_ready = sem("h_ready")
        w_ready = sem("w_ready")
        msg_ready = sem("msg_ready")
        same_ready = sem("same_ready")
        dumped_ready = sem("dumped_ready")
        agg_idx_ready = sem("agg_idx_ready")
        sump_ready = sem("sump_ready")
        sums_ready = sem("sums_ready")
        atp_ready = sem("atp_ready")
        at_ready = sem("at_ready")
        z2_ready = sem("z2_ready")
        abs2_ready = sem("abs2_ready")
        e2_ready = sem("e2_ready")
        l2_ready = sem("l2_ready")
        s2_ready = sem("s2_ready")
        y_ready = sem("y_ready")
        xy_ready = sem("xy_ready")
        stat_step = sem("stat_step")
        var_ready = sem("var_ready")
        lnvar_ready = sem("lnvar_ready")
        rough_ready = sem("rough_ready")
        norm_step = sem("norm_step")
        rstd_ready = sem("rstd_ready")
        norm_ready = sem("norm_ready")
        rows_ready = sem("rows_ready")
        normalise_turns = sem("normalise_turns")

        N_WEIGHTS = 9

        def batch(k, s, q, back):
            n = Q * s + q - back
            turns = n // (Q * NS)
            n -= turns * Q * NS
            return NS * (k + turns) + n // Q, n // Q, n % Q, Q * NS * (k + turns) + n

        def b_slot(s, q):
            return (Q * s + q) % 2

        def real(*at_batch):
            return not isinstance(at_batch[3], int) or at_batch[3] >= 0

        def node_loop(engine, step):
            for s in range(NS):
                for q in range(Q):
                    step(0, s, q)
            with engine.Fori(1, KN) as k:
                for s in range(NS):
                    for q in range(Q):
                        step(k, s, q)
            for q in range(Q):
                step(KN, 0, q)

        LAST = (KN, 0, Q - 1)
        REST = Q * NCH
        RS, RB = 1, REST % 2

        block = ctx.enter_context(nc.Block())

        @block.sync
        def _(sp):
            for j in range(U):
                sp.dma_start(dst_idx[j][:, :], dstT[:, j * T:(j + 1) * T]).then_inc(dst_in[j], 16)
                sp.dma_start(attr[j][:, :], attrT[:, j * GE:(j + 1) * GE]).then_inc(attr_in[j], 16)
            for t, a in ((w_f1, W_f1), (w_in, W_in2f), (w_f2, W_f2), (w_o1, W_o1), (w_o2, W_o2)):
                sp.dma_start(t[:, :], a).then_inc(weights_in, 16)
            sp.dma_start(bf1_col[:, :], b_f1.rearrange("(p a) -> p a", a=1)).then_inc(weights_in, 16)
            sp.dma_start(bo1_col[:, :], b_o1.rearrange("(p a) -> p a", a=1)).then_inc(weights_in, 16)
            sp.dma_start(b_rows[:, 0, :], b_f2.rearrange("(a n) -> a n", a=1)).then_inc(weights_in, 16)
            sp.dma_start(b_rows[:, 1, :], b_o2.rearrange("(a n) -> a n", a=1)).then_inc(weights_in, 16)
            sp.dma_start(weight[:, :], weightT).then_inc(edges_in, 16)
            sp.dma_start(src_col[:, :], srcT).then_inc(edges_in, 16)
            for j in range(U):
                sp.dma_start(src_row[j][:, :], src[j * GE:(j + 1) * GE].partition_broadcast(128)).then_inc(src_in[j], 16)
            sp.wait_ge(c_parts_ready, 1)
            for k in range(2):
                for t in range(T):
                    sp.dma_start(c3[:, k, t, :], c_parts[0:1, k, :, :]).then_inc(c3_in, 16)

            def next_front(i, j):
                sp.wait_ge(xg_in[j], 16 * T * (i + 1))
                sp.dma_start(dst_idx[j][:, :], dstT[:, bass.ds((i + 1) * U * T + j * T, T)]).then_inc(dst_in[j], 16)
                sp.wait_ge(z1_ready, U * i + j + 1)
                sp.dma_start(attr[j][:, :], attrT[:, bass.ds((i + 1) * U * GE + j * GE, GE)]).then_inc(attr_in[j], 16)

            def next_back(i, j):
                sp.wait_ge(same_ready, U * i + j + 1)
                sp.dma_start(src_row[j][:, :],
                             src[bass.ds((i + 1) * U * GE + j * GE, GE)].partition_broadcast(128)).then_inc(src_in[j], 16)

            zero_ch = agg_dram[0:NZ * 128 * ZN, :].rearrange("(p c) f -> p (c f)", p=128)
            sp.wait_ge(zeros_set, 1)
            sp.dma_start(agg_dram[NZ * 128 * ZN:N + DUMP, :].rearrange("(p c) f -> p (c f)", c=ZN),
                         zeros[0:ZREST // ZN, :]).then_inc(zeroed, 16)

            def zero(n):
                sp.dma_start(zero_ch[:, bass.ds(n * ZN * F, ZN * F)], zeros[:, :]).then_inc(zeroed, 16)

            for n in range(NZ % LAG):
                zero(n)
            with sp.Fori(0, LAG) as i:
                for j in range(U):
                    for n in range(j * (NZ // LAG) // U, (j + 1) * (NZ // LAG) // U):
                        zero(i * (NZ // LAG) + NZ % LAG + n)
                    next_front(i, j)
            with sp.Fori(LAG, NI - 1) as i:
                for j in range(U):
                    next_front(i, j)
                    next_back(i - LAG, j)
            with sp.Fori(NI - 1, NI - 1 + LAG) as i:
                for j in range(U):
                    next_back(i - LAG, j)

            def load_x(c, s):
                sp.dma_start(xn[s][:, :, :].rearrange("p c f -> p (c f)"),
                             x_ch[:, bass.ds(c * CN * F, CN * F)]).then_inc(xn_in[s], 16)

            def load_agg(c, s):
                sp.dma_start(an[s][:, :, :].rearrange("p c f -> p (c f)"),
                             agg_ch[:, bass.ds(c * CN * F, CN * F)]).then_inc(an_in[s], 16)

            def store(c, s):
                sp.dma_start(out_ch[:, bass.ds(c * CN * F, CN * F)],
                             rows_out[s][:, :, :].rearrange("p c f -> p (c f)")).then_inc(out_done[s], 16)

            def step(c, s):
                if not isinstance(c, int) or c >= 2:
                    sp.wait_ge(rows_ready, c - 1)
                    store(c - 2, (s - 2) % NS)
                    if not isinstance(c, int) or c + 2 < NCH:
                        load_x(c + 2, (s + 2) % NS)
                sp.wait_ge(atp_ready, Q * (c + 1))
                if not isinstance(c, int) or c + 4 < NCH:
                    load_agg(c + 4, s)

            for s in range(NS):
                load_x(s, s)
            sp.wait_ge(added, 16 * NTILES)
            for s in range(NS):
                load_agg(s, s)
            for s in range(NS):
                step(s, s)
            with sp.Fori(1, KN - 1) as k:
                for s in range(NS):
                    step(NS * k + s, s)
            for s in range(NS):
                step(NS * (KN - 1) + s, s)
                if s == RS:
                    sp.dma_start(an[RS][0:TP, 0:TN, :].rearrange("p c f -> p (c f)"), rest(agg_dram)).then_inc(an_in[RS], 16)
            step(NCH - 1, 0)
            sp.dma_start(xn[RS][0:TP, 0:TN, :].rearrange("p c f -> p (c f)"), rest(x)).then_inc(xn_in[RS], 16)
            sp.wait_ge(rows_ready, NCH - 1)
            store(NCH - 2, (NCH - 2) % NS)
            sp.wait_ge(rows_ready, NCH)
            store(NCH - 1, 0)
            sp.wait_ge(rows_ready, NCH + 1)
            sp.dma_start(rest(out), rows_out[RS][0:TP, 0:TN, :].rearrange("p c f -> p (c f)")).then_inc(out_done[RS], 16)
            for s in range(NS):
                sp.wait_ge(out_done[s], 16 * (KN + (s in (0, RS))))

        @block.gpsimd
        def _(pool):
            def gather(i, j, tiles):
                for t in tiles:
                    pool.indirect_dma_start(
                        out=xg[j][:, t, :], out_offset=None, in_=x,
                        in_offset=bass.IndirectOffsetOnAxis(ap=dst_idx[j][:, t:t + 1], axis=0),
                    ).then_inc(xg_in[j], 16)

            def ready_to_gather(i, j):
                pool.wait_ge(dst_in[j], 16 * (i + 1))
                wait(pool, xtp_ready, U * (i - 1) + j + 1)
                pool.sem_inc(gather_turns, 1)

            def add_pair(i, j, pair):
                wait(pool, added, 16 * (T * (U * i + j) + 2 * pair))
                pool.wait_ge(agg_idx_ready, U * i + j + 1)
                pool.wait_ge(sums_ready, U * i + j + 1)
                pool.sem_inc(add_turns, 1)
                for t in (2 * pair, 2 * pair + 1):
                    pool.indirect_dma_start(
                        out=agg_dram, in_=sums[j][:, t, :], in_offset=None,
                        out_offset=bass.IndirectOffsetOnAxis(ap=agg_idx[j][:, t:t + 1], axis=0),
                        compute_op=ALU.add,
                    ).then_inc(added, 16)

            nc.gpsimd.memset(ident[:, :], 0.0).then_inc(pool_consts, 1)
            nc.gpsimd.memset(not_after[:, :], 1.0).then_inc(pool_consts, 1)
            ready_to_gather(0, 0)
            gather(0, 0, range(T))
            pool.wait_ge(pool_consts, 2)
            pool.affine_select(out=ident[:, :], in_=ident[:, :], compare_op=ALU.not_equal, fill=1.0,
                               base=0, pattern=[[-1, 128]], channel_multiplier=1).then_inc(pool_consts, 1)
            pool.affine_select(out=not_after[:, :], in_=not_after[:, :], compare_op=ALU.is_ge, fill=0.0,
                               base=TE, pattern=[[-1, 2 * TE]], channel_multiplier=1).then_inc(pool_consts, 1)
            pool.iota(dump_i[:, :], pattern=[[TE, T]], base=N, channel_multiplier=1).then_inc(pool_consts, 1)
            for j in range(1, U):
                ready_to_gather(0, j)
                gather(0, j, range(T))
            with pool.Fori(1, LAG + 1) as i:
                for j in range(U):
                    ready_to_gather(i, j)
                    gather(i, j, range(T))
            pool.wait_ge(zeroed, 16 * (NZ + 1))
            pool.sem_inc(add_turns, 1)

            def gather_and_add(i, j):
                for pair in range(2):
                    if pair == 0:
                        ready_to_gather(i + 1, j)
                    gather(i + 1, j, (2 * pair, 2 * pair + 1))
                    add_pair(i - LAG, j, pair)

            for j in range(U):
                gather_and_add(LAG, j)
            with pool.Fori(LAG + 1, NI - 1) as i:
                for j in range(U):
                    gather_and_add(i, j)
            with pool.Fori(NI - 1, NI + LAG) as i:
                for j in range(U):
                    for pair in range(2):
                        add_pair(i - LAG, j, pair)

            def normalise(c, s, stores, P=128, C=CN):
                wait(pool, out_done[s], 16 * stores)
                pool.wait_ge(norm_ready, c + 1)
                pool.sem_inc(normalise_turns, 1)
                for r in range(C):
                    last = nc.gpsimd.tensor_scalar(rows_out[s][0:P, r, :], xn[s][0:P, r, :], rstd[s % 2][0:P, r:r + 1],
                                                   nmr[s % 2][0:P, r:r + 1], ALU.mult, ALU.add)
                last.then_inc(rows_ready, 1)

            for s in range(NS):
                normalise(s, s, 0)
            with pool.Fori(1, KN) as k:
                for s in range(NS):
                    normalise(NS * k + s, s, k)
            normalise(NCH - 1, 0, KN)
            normalise(NCH, RS, KN, TP, TN)

        @block.tensor
        def _(pe):
            pe.wait_ge(weights_in, 16 * N_WEIGHTS)
            pe.wait_ge(dve_consts, 1)
            nc.tensor.matmul(c_ps[0:1, 0:F], left_f1[:, :], w_f2[:, :], start=True, stop=True)
            nc.tensor.matmul(c_ps[0:1, F:2 * F], left_o1[:, :], w_o2[:, :], start=True, stop=True).then_inc(left_ready, 1)
            pe.wait_ge(pool_consts, 5)
            pe.wait_ge(c3_in, 16 * 2 * T)

            def filter_in(i, j):
                n = U * i + j
                pe.wait_ge(attr_in[j], 16 * (i + 1))
                wait(pe, s1_ready, n)
                nc.tensor.matmul(z1_ps[:, 0:GE], w_f1[:, :], attr[j][:, :], start=True, stop=True).then_inc(z1_ready, 1)
                pe.wait_ge(xg_in[j], 16 * T * (i + 1))
                wait(pe, xt_ready, n)
                for t in range(T):
                    last = nc.tensor.transpose(xt_ps[:, t * TE:(t + 1) * TE], xg[j][:, t, :], ident[0:TE, 0:TE])
                last.then_inc(xtp_ready, 1)

            def message(i, j):
                n = U * i + j
                pe.wait_ge(xt_ready, n + 1)
                wait(pe, h_ready, n)
                for t in range(T):
                    last = nc.tensor.matmul(h_ps[0:TE, t * F:(t + 1) * F], xt[j % 2][:, t * TE:(t + 1) * TE],
                                            w_in[:, :], start=True, stop=True)
                last.then_inc(hp_ready, 1)
                wait(pe, msg_ready, n)
                pe.wait_ge(s1_ready, n + 1)
                nc.tensor.matmul(w_ps[0:TE, :], ones3[:, 0:TE], c3[:, 0, :, :].rearrange("p t f -> p (t f)"),
                                 start=True, stop=False, skip_group_check=True)
                for t in range(T):
                    last = nc.tensor.matmul(w_ps[0:TE, t * F:(t + 1) * F], s1[j % 2][:, t * TE:(t + 1) * TE], w_f2[:, :],
                                            start=False, stop=(t == T - 1), skip_group_check=True)
                last.then_inc(w_ready, 1)

            def sum_pairs(i, j):
                n = U * i + j
                pe.wait_ge(same_ready, n + 1)
                wait(pe, sums_ready, n)
                ring = (i % RING) * (U * T * F) + j * T * F
                for pair in range(2):
                    t0, t1 = 2 * pair, 2 * pair + 1
                    m0, m1 = (msg[0:TE, bass.ds(ring + t * F, F)] for t in (t0, t1))
                    eq = same[j % 2][:, pair, :]
                    nc.tensor.matmul(sum_ps[0:TE, t0 * F:(t0 + 1) * F], eq[:, 0:TE], m0, start=True, stop=False)
                    nc.tensor.matmul(sum_ps[0:TE, t0 * F:(t0 + 1) * F], eq[:, TE:2 * TE], m1, start=False, stop=True)
                    last = nc.tensor.matmul(sum_ps[0:TE, t1 * F:(t1 + 1) * F], eq[:, 2 * TE:3 * TE], m1,
                                            start=True, stop=True)
                last.then_inc(sump_ready, 1)

            filter_in(0, 0)
            for j in range(U):
                filter_in(*after(0, j))
                message(0, j)
            with pe.Fori(1, LAG) as i:
                for j in range(U):
                    filter_in(*after(i, j))
                    message(i, j)

            def both(i, j):
                filter_in(*after(i, j))
                message(i, j)
                sum_pairs(i - LAG, j)

            for j in range(U):
                both(LAG, j)
            with pe.Fori(LAG + 1, NI - 1) as i:
                for j in range(U):
                    both(i, j)
            for j in range(U):
                if j + 1 < U:
                    filter_in(NI - 1, j + 1)
                message(NI - 1, j)
                sum_pairs(NI - 1 - LAG, j)
            with pe.Fori(NI, NI + LAG) as i:
                for j in range(U):
                    sum_pairs(i - LAG, j)

            pe.wait_ge(sums_ready, NI * U)

            def transpose_agg(c, s, q, b, k, P=128, tiles=4):
                pe.wait_ge(an_in[s], 16 * (k + 1))
                wait(pe, at_ready, b - 1)
                for t in range(tiles):
                    last = nc.tensor.transpose(at_ps[b_slot(s, q)][:, t * P:(t + 1) * P], an[s][0:P, 4 * q + t, :],
                                               ident[0:P, 0:P])
                last.then_inc(atp_ready, 1)

            def hidden(c, s, q, b, W=512):
                pe.wait_ge(at_ready, b + 1)
                wait(pe, s2_ready, b - 1)
                p = b_slot(s, q)
                nc.tensor.matmul(z2_ps[p][:, 0:W], w_o1[:, :], at[p][:, 0:W], start=True, stop=True).then_inc(z2_ready, 1)

            def update(c, s, q, b, P=128, tiles=4):
                pe.wait_ge(s2_ready, b + 1)
                wait(pe, xy_ready, b - 1)
                p = b_slot(s, q)
                nc.tensor.matmul(y_ps[p][0:P, 0:tiles * F], ones3[:, 0:P], c3[:, 1, 0:tiles, :].rearrange("p t f -> p (t f)"),
                                 start=True, stop=False, skip_group_check=True)
                for t in range(tiles):
                    last = nc.tensor.matmul(y_ps[p][0:P, t * F:(t + 1) * F], s2[p][:, t * P:(t + 1) * P], w_o2[:, :],
                                            start=False, stop=(t == tiles - 1), skip_group_check=True)
                last.then_inc(y_ready, 1)

            def step(k, s, q):
                transpose_agg(*batch(k, s, q, 0), k)
                for stage, back in ((hidden, 1), (update, 3)):
                    if real(*batch(k, s, q, back)):
                        stage(*batch(k, s, q, back))

            node_loop(pe, step)
            the_rest = (NCH, RS, 0, REST)
            transpose_agg(*the_rest, KN, TP, TN)
            hidden(*batch(*LAST, 0))
            update(*batch(*LAST, 2))
            hidden(*the_rest, TP * TN)
            update(*batch(*LAST, 1))
            update(*batch(*LAST, 0))
            update(*the_rest, TP, TN)

        @block.scalar
        def _(act):
            act.preload_act_table_set("natural_log_exp_and_others")

            act.wait_ge(weights_in, 16 * N_WEIGHTS)

            def abs1(i, j):
                n = U * i + j
                act.wait_ge(z1_ready, n + 1)
                wait(act, s1_ready, n)
                nc.scalar.activation(e1[:, :], z1_ps[:, 0:GE], ACT.Abs, bias=bf1_col[:, :]).then_inc(abs1_ready, 1)

            def exp1(i, j):
                act.wait_ge(abs1_ready, U * i + j + 1)
                nc.scalar.activation(e1[:, :], e1[:, :], ACT.Exp, scale=-1.0).then_inc(e1_ready, 1)

            def copy_xt(i, j):
                n = U * i + j
                act.wait_ge(xtp_ready, n + 1)
                wait(act, hp_ready, n - 1)
                nc.scalar.activation(xt[j % 2][:, :], xt_ps[:, 0:GE], ACT.Copy).then_inc(xt_ready, 1)

            def copy_h(i, j):
                n = U * i + j
                act.wait_ge(hp_ready, n + 1)
                wait(act, msg_ready, n)
                nc.scalar.activation(h[:, :, :].rearrange("p t f -> p (t f)"), h_ps[0:TE, :],
                                     ACT.Copy).then_inc(h_ready, 1)

            def ln1(i, j):
                act.wait_ge(e1_ready, U * i + j + 1)
                nc.scalar.activation(e1[:, :], e1[:, :], ACT.Ln, bias=1.0).then_inc(l1_ready, 1)

            def copy_sums(i, j):
                n = U * i + j
                act.wait_ge(sump_ready, n + 1)
                wait(act, added, 16 * T * (n - U + 1))
                nc.scalar.activation(sums[j][:, :, :].rearrange("p t f -> p (t f)"), sum_ps[0:TE, :],
                                     ACT.Copy).then_inc(sums_ready, 1)

            def front(i, j):
                abs1(*after(i, j))
                exp1(*after(i, j))
                copy_xt(*after(i, j))
                ln1(*after(i, j))
                copy_h(i, j)

            def both(i, j):
                front(i, j)
                copy_sums(i - LAG, j)

            abs1(0, 0)
            exp1(0, 0)
            copy_xt(0, 0)
            ln1(0, 0)
            for j in range(U):
                front(0, j)
            with act.Fori(1, LAG) as i:
                for j in range(U):
                    front(i, j)
            for j in range(U):
                both(LAG, j)
            with act.Fori(LAG + 1, NI - 1) as i:
                for j in range(U):
                    both(i, j)
            for j in range(U):
                if j + 1 < U:
                    front(NI - 1, j)
                else:
                    copy_h(NI - 1, j)
                copy_sums(NI - 1 - LAG, j)
            with act.Fori(NI, NI + LAG) as i:
                for j in range(U):
                    copy_sums(i - LAG, j)

            def copy_at(c, s, q, b, W=512):
                p = b_slot(s, q)
                act.wait_ge(atp_ready, b + 1)
                wait(act, z2_ready, b - 1)
                nc.scalar.activation(at[p][:, 0:W], at_ps[p][:, 0:W], ACT.Copy).then_inc(at_ready, 1)

            def abs2(c, s, q, b, W=512):
                p = b_slot(s, q)
                act.wait_ge(z2_ready, b + 1)
                wait(act, s2_ready, b - 1)
                nc.scalar.activation(e2[p][:, 0:W], z2_ps[p][:, 0:W], ACT.Abs, bias=bo1_col[:, :]).then_inc(abs2_ready, 1)

            def exp2(c, s, q, b, W=512):
                p = b_slot(s, q)
                act.wait_ge(abs2_ready, b + 1)
                nc.scalar.activation(e2[p][:, 0:W], e2[p][:, 0:W], ACT.Exp, scale=-1.0).then_inc(e2_ready, 1)

            def ln2(c, s, q, b, W=512):
                p = b_slot(s, q)
                act.wait_ge(e2_ready, b + 1)
                nc.scalar.activation(e2[p][:, 0:W], e2[p][:, 0:W], ACT.Ln, bias=1.0).then_inc(l2_ready, 1)

            def rough_rstd(c, s, P=128, C=CN):
                r0 = rstd0[s % 2][0:P, 0:C]
                act.wait_ge(var_ready, c + 1)
                nc.scalar.activation(r0, var[s % 2][0:P, 0:C], ACT.Ln).then_inc(lnvar_ready, 1)
                act.wait_ge(lnvar_ready, c + 1)
                nc.scalar.activation(r0, r0, ACT.Exp, scale=-0.5).then_inc(rough_ready, 1)

            def step(k, s, q):
                for stage, back in ((abs2, 1), (ln2, 2), (exp2, 1), (copy_at, 0)):
                    if real(*batch(k, s, q, back)):
                        stage(*batch(k, s, q, back))
                c, cs, cq, b = batch(k, s, q, 4)
                if cq == Q - 1 and real(c, cs, cq, b):
                    rough_rstd(c, cs)

            node_loop(act, step)
            the_rest = (NCH, RS, 0, REST)
            abs2(*batch(*LAST, 0))
            ln2(*batch(*LAST, 1))
            exp2(*batch(*LAST, 0))
            copy_at(*the_rest, TP * TN)
            rough_rstd(NCH - 2, NS - 1)
            abs2(*the_rest, TP * TN)
            exp2(*the_rest, TP * TN)
            ln2(*batch(*LAST, 0))
            ln2(*the_rest, TP * TN)
            rough_rstd(NCH - 1, 0)
            rough_rstd(NCH, RS, TP, TN)

        @block.vector
        def _(dve):
            nc.vector.memset(zeros[:, :], 0.0).then_inc(zeros_set, 1)
            nc.vector.memset(ones3[:, :], 1.0)
            dve.wait_ge(weights_in, 16 * N_WEIGHTS)
            nc.vector.tensor_scalar(neg_bf1[:, :], bf1_col[:, :], -1.0, None, ALU.mult)
            nc.vector.tensor_scalar(neg_bo1[:, :], bo1_col[:, :], -1.0, None, ALU.mult)
            nc.vector.tensor_scalar(left_f1[:, :], bf1_col[:, :], -LOG2, None, ALU.add)
            nc.vector.tensor_scalar(left_o1[:, :], bo1_col[:, :], -LOG2, None, ALU.add).then_inc(dve_consts, 1)
            dve.wait_ge(left_ready, 1)
            nc.vector.tensor_tensor(c_rows[:, :, :], c_ps[0:1, 0:2 * F].rearrange("p (k f) -> p k f", k=2),
                                    b_rows[:, :, :], ALU.add).then_inc(split_step, 1)
            for part in range(3):
                dve.wait_ge(split_step, 1 + 2 * part)
                nc.vector.tensor_copy(c_parts[:, :, part, :], c_rows[:, :, :]).then_inc(
                    c_parts_ready if part == 2 else split_step, 1)
                if part < 2:
                    dve.wait_ge(split_step, 2 + 2 * part)
                    nc.vector.tensor_tensor(c_rows[:, :, :], c_rows[:, :, :], c_parts[:, :, part, :],
                                            ALU.subtract).then_inc(split_step, 1)
            dve.wait_ge(edges_in, 16 * 2)
            nc.vector.tensor_copy(src_f[:, :], src_col[:, :]).then_inc(dve_consts, 1)
            dve.wait_ge(pool_consts, 5)
            nc.vector.tensor_copy(dump[:, :], dump_i[:, :]).then_inc(dve_consts, 1)
            dve.wait_ge(dve_consts, 3)

            def softplus1(i, j):
                n = U * i + j
                dve.wait_ge(l1_ready, n + 1)
                wait(dve, w_ready, n - 1)
                nc.vector.scalar_tensor_tensor(s1[j % 2][:, :], z1_ps[:, 0:GE], neg_bf1[:, :], e1[:, :],
                                               ALU.max, ALU.add).then_inc(s1_ready, 1)

            def message(i, j):
                dve.wait_ge(h_ready, U * i + j + 1)
                dve.wait_ge(w_ready, U * i + j + 1)
                ring = (i % RING) * (U * T * F) + j * T * F
                for t in range(T):
                    last = nc.vector.scalar_tensor_tensor(
                        msg[0:TE, bass.ds(ring + t * F, F)], w_ps[0:TE, t * F:(t + 1) * F],
                        weight[:, bass.ds(U * T * i + T * j + t, 1)], h[:, t, :], ALU.mult, ALU.mult)
                last.then_inc(msg_ready, 1)

            def mark(i, j):
                n = U * i + j
                dve.wait_ge(src_in[j], 16 * (i + 1))
                wait(dve, sump_ready, n - 1)
                for pair in range(2):
                    for t, cols in ((0, TE), (1, 2 * TE)):
                        tile = 2 * pair + t
                        last = nc.vector.scalar_tensor_tensor(
                            same[j % 2][:, pair, TE * t:TE * t + cols],
                            src_row[j][0:TE, 2 * TE * pair:2 * TE * pair + cols],
                            src_f[:, bass.ds(U * T * i + T * j + tile, 1)],
                            not_after[:, 2 * TE - cols:2 * TE], ALU.is_equal, ALU.mult,
                            accum_out=rank[j % 2][:, tile:tile + 1])
                last.then_inc(same_ready, 1)

            def index(i, j):
                n = U * i + j
                dve.wait_ge(same_ready, n + 1)
                nc.vector.scalar_tensor_tensor(dumped[:, :], rank[j % 2][:, :], 1.5, dump[:, :],
                                               ALU.is_gt, ALU.mult).then_inc(dumped_ready, 1)
                dve.wait_ge(dumped_ready, n + 1)
                wait(dve, added, 16 * T * (n - U + 1))
                nc.vector.tensor_tensor(agg_idx[j][:, :], dumped[:, :], src_f[:, bass.ds(U * T * i + T * j, T)],
                                        ALU.max).then_inc(agg_idx_ready, 1)

            def front(i, j):
                softplus1(*after(i, j))
                message(i, j)

            def both(i, j):
                mark(i - LAG, j)
                softplus1(*after(i, j))
                index(i - LAG, j)
                message(i, j)

            softplus1(0, 0)
            for j in range(U):
                front(0, j)
            with dve.Fori(1, LAG) as i:
                for j in range(U):
                    front(i, j)
            for j in range(U):
                both(LAG, j)
            with dve.Fori(LAG + 1, NI - 1) as i:
                for j in range(U):
                    both(i, j)
            for j in range(U):
                mark(NI - 1 - LAG, j)
                if j + 1 < U:
                    softplus1(NI - 1, j + 1)
                index(NI - 1 - LAG, j)
                message(NI - 1, j)
            with dve.Fori(NI, NI + LAG) as i:
                for j in range(U):
                    mark(i - LAG, j)
                    index(i - LAG, j)

            def softplus2(c, s, q, b, W=512):
                p = b_slot(s, q)
                dve.wait_ge(l2_ready, b + 1)
                wait(dve, y_ready, b - 1)
                nc.vector.scalar_tensor_tensor(s2[p][:, 0:W], z2_ps[p][:, 0:W], neg_bo1[:, :], e2[p][:, 0:W],
                                               ALU.max, ALU.add).then_inc(s2_ready, 1)

            def residual(c, s, q, b, loads, P=128, tiles=4):
                rows = xn[s][0:P, 4 * q:4 * q + tiles, :]
                if q == 0:
                    dve.wait_ge(xn_in[s], 16 * loads)
                dve.wait_ge(y_ready, b + 1)
                nc.vector.tensor_tensor(rows, y_ps[b_slot(s, q)][0:P, 0:tiles * F].rearrange("p (t f) -> p t f", t=tiles),
                                        rows, ALU.add).then_inc(xy_ready, 1)
                dve.wait_ge(xy_ready, b + 1)
                for r in range(4 * q, 4 * q + tiles):
                    last = nc.vector.bn_stats(stats[0:P, r, :], xn[s][0:P, r, :])
                return last

            def moments(c, s, P=128, C=CN):
                mean_e, m2_e, mean_o, m2_o = (stats[0:P, 0:C, m] for m in (1, 2, 4, 5))
                dve.wait_ge(stat_step, 4 * c + 1)
                nc.vector.tensor_tensor(dmean[0:P, 0:C], mean_e, mean_o, ALU.subtract)
                nc.vector.tensor_tensor(msum[s % 2][0:P, 0:C], mean_e, mean_o, ALU.add)
                nc.vector.tensor_tensor(m2[0:P, 0:C], m2_e, m2_o, ALU.add).then_inc(stat_step, 1)
                dve.wait_ge(stat_step, 4 * c + 2)
                nc.vector.tensor_tensor(dmean[0:P, 0:C], dmean[0:P, 0:C], dmean[0:P, 0:C], ALU.mult).then_inc(stat_step, 1)
                dve.wait_ge(stat_step, 4 * c + 3)
                nc.vector.scalar_tensor_tensor(m2[0:P, 0:C], dmean[0:P, 0:C], F / 4.0, m2[0:P, 0:C],
                                               ALU.mult, ALU.add).then_inc(stat_step, 1)
                dve.wait_ge(stat_step, 4 * c + 4)
                wait(dve, rstd_ready, c - 1)
                nc.vector.tensor_scalar(var[s % 2][0:P, 0:C], m2[0:P, 0:C], 1.0 / F, EPS,
                                        ALU.mult, ALU.add).then_inc(var_ready, 1)

            def refine(c, s, P=128, C=CN):
                r0, r, v = (a[s % 2][0:P, 0:C] for a in (rstd0, rstd, var))
                dve.wait_ge(rough_ready, c + 1)
                nc.vector.tensor_tensor(newton[0:P, 0:C], r0, r0, ALU.mult).then_inc(norm_step, 1)
                dve.wait_ge(norm_step, 2 * c + 1)
                nc.vector.scalar_tensor_tensor(newton[0:P, 0:C], newton[0:P, 0:C], -0.5, v,
                                               ALU.mult, ALU.mult).then_inc(norm_step, 1)
                dve.wait_ge(norm_step, 2 * c + 2)
                wait(dve, rows_ready, c - 1)
                nc.vector.scalar_tensor_tensor(r, newton[0:P, 0:C], 1.5, r0, ALU.add, ALU.mult).then_inc(rstd_ready, 1)
                dve.wait_ge(rstd_ready, c + 1)
                nc.vector.scalar_tensor_tensor(nmr[s % 2][0:P, 0:C], msum[s % 2][0:P, 0:C], -0.5, r,
                                               ALU.mult, ALU.mult).then_inc(norm_ready, 1)

            def sum_up(k, s, q):
                c, cs, cq, b = batch(k, s, q, 3)
                if real(c, cs, cq, b):
                    turn = k if Q * s + q >= 3 else k - 1
                    last = residual(c, cs, cq, b, turn + 1)
                    if cq == Q - 1:
                        last.then_inc(stat_step, 1)
                        moments(c, cs)
                c, cs, cq, b = batch(k, s, q, 5)
                if cq == Q - 1 and real(c, cs, cq, b):
                    refine(c, cs)

            def step(k, s, q):
                if real(*batch(k, s, q, 2)):
                    softplus2(*batch(k, s, q, 2))
                sum_up(k, s, q)

            node_loop(dve, step)
            the_rest = (NCH, RS, 0, REST)
            softplus2(*batch(*LAST, 1))
            residual(*batch(*LAST, 2), KN + 1)
            softplus2(*batch(*LAST, 0))
            residual(*batch(*LAST, 1), KN + 1)
            refine(NCH - 2, NS - 1)
            softplus2(*the_rest, TP * TN)
            residual(*batch(*LAST, 0), KN + 1).then_inc(stat_step, 1)
            moments(NCH - 1, 0)
            residual(*the_rest, KN + 1, TP, TN).then_inc(stat_step, 1)
            moments(NCH, RS, TP, TN)
            refine(NCH - 1, 0)
            refine(NCH, RS, TP, TN)


def kernel(x, src, dst, edge_attr_20, edge_weight, L0_gnn_W_in2f, L0_gnn_W_f1, L0_gnn_b_f1, L0_gnn_W_f2,
           L0_gnn_b_f2, L0_gnn_W_o1, L0_gnn_b_o1, L0_gnn_W_o2, L0_gnn_b_o2):
    import numpy as _np
    import concourse.bacc as _bacc
    from concourse import mybir as _mybir
    from concourse.bass_utils import run_bass_kernel_spmd as _run

    TILE = 125

    def tiled(a):
        return _np.ascontiguousarray(_np.asarray(a).reshape(-1, TILE).T)

    arrays = {
        "x": x, "dstT": tiled(dst), "src": src, "srcT": tiled(src),
        "attrT": _np.asarray(edge_attr_20).T, "weightT": tiled(edge_weight),
        "W_in2f": L0_gnn_W_in2f, "W_f1": L0_gnn_W_f1, "b_f1": L0_gnn_b_f1, "W_f2": L0_gnn_W_f2,
        "b_f2": L0_gnn_b_f2, "W_o1": L0_gnn_W_o1, "b_o1": L0_gnn_b_o1, "W_o2": L0_gnn_W_o2, "b_o2": L0_gnn_b_o2,
    }
    arrays = {k: _np.ascontiguousarray(v) for k, v in arrays.items()}
    nc = _bacc.Bacc("TRN2", target_bir_lowering=False, num_devices=1)
    args = [nc.dram_tensor(k, a.shape, _mybir.dt.from_np(a.dtype), kind="ExternalInput").ap()
            for k, a in arrays.items()]
    out = nc.dram_tensor("out", arrays["x"].shape, _mybir.dt.float32, kind="ExternalOutput").ap()
    gnn_resnorm_kernel(nc, *args, out)
    r = _run(nc, [arrays], core_ids=[0])
    return r.results[0]["out"]
```

```python
import concourse.bass as bass
from concourse import mybir
from contextlib import ExitStack



def gnn_resnorm_kernel(nc, x, dstT, src, srcT, attrT, weightT, W_in2f, W_f1, b_f1, W_f2, b_f2,
                       W_o1, b_o1, W_o2, b_o2, out):
    f32, bf16, i32 = mybir.dt.float32, mybir.dt.bfloat16, mybir.dt.int32
    ALU = mybir.AluOpType
    ACT = mybir.ActivationFunctionType

    N, F = x.shape
    R, E = attrT.shape
    TE, NTILES = dstT.shape
    T = 4
    GE = T * TE
    NG = E // GE
    U = 4
    V = 8
    V0 = 2
    VS = 4
    NI = -(-NG // U)
    UL = NG - (NI - 1) * U
    LEAD = 12
    NM = NI - LEAD
    assert 1 < UL <= U and NG * GE == E and NTILES * TE == E and F == TE == 128
    MIX = tuple((j, (2 * j, 2 * j + 1)) for j in range(U))
    FIRST_BACKS, FIRST_MIX = (V0, V0 + 1), tuple((j, (V0 + 2 + j,)) for j in range(U))
    LAST_BACKS = NG + V0 - V * (NM - 1)
    LAST_MIX = ((0, (0, 1)),) + tuple((j, (j + 1,)) for j in range(1, UL))
    RING = (LEAD + 1) * U
    assert V == 2 * U == V0 + 2 + U and V % VS == 0 and V0 % 2 == 0 and LAST_BACKS == V0 + UL
    DUMP = GE

    CN = 12
    Q = CN // 4
    NCH = N // (128 * CN)
    NPP = NCH * CN
    ND = 128 * NPP
    TP, TN = 80, 2
    assert ND + TP * TN == N
    NS = 4
    KN = NCH // NS
    AR, AR_LAST, AR_REST = 1, 6, 1
    assert Q * NS % 6 == 0
    assert NCH == KN * NS + 1

    LOG2 = 0.6931471805599453
    EPS = 1e-5
    assert N + DUMP < (1 << 24)

    agg_dram = nc.dram_tensor("agg_dram", [N + DUMP, F], f32, kind="Internal").ap()
    ZN = 13
    NZ = (N + DUMP) // (128 * ZN)
    ZP, ZR = 56, 12
    assert NZ * 128 * ZN + ZP * ZR == N + DUMP and ZR <= ZN and NZ % LEAD == 0

    def chunked(a):
        return a[0:ND, :].rearrange("(p c) f -> p (c f)", c=NPP)

    def rest(a):
        return a[ND:N, :].rearrange("(p c) f -> p (c f)", c=TN)

    x_ch, agg_ch, out_ch = chunked(x), chunked(agg_dram), chunked(out)

    def wait(engine, semaphore, count):
        if not isinstance(count, int) or count > 0:
            engine.wait_ge(semaphore, count)

    def after(i, j):
        return (i, j + 1) if j + 1 < U else (i + 1, 0)

    def before(i, j):
        return (i, j - 1) if j > 0 else (i - 1, U - 1)

    ctx = ExitStack()
    with ctx:
        def sb(name, shape, dt=f32):
            return ctx.enter_context(nc.sbuf_tensor(name, shape, dt))

        def sem(name):
            return ctx.enter_context(nc.semaphore(name))

        w_in = sb("w_in", [F, F])
        w_f1 = sb("w_f1", [R, F])
        w_f2 = sb("w_f2", [F, F])
        w_o1 = sb("w_o1", [F, F])
        w_o2 = sb("w_o2", [F, F])
        bf1_col = sb("bf1_col", [F, 1])
        bo1_col = sb("bo1_col", [F, 1])
        bf2_col = sb("bf2_col", [F, 1])
        bo2_row = sb("bo2_row", [1, F])
        cf_col = sb("cf_col", [F, 1])
        c_rows = sb("c_rows", [1, 2, F])
        c_parts = sb("c_parts", [1, 2, 3, F], bf16)
        c3 = sb("c3", [3, 2, T, F], bf16)
        ones3 = sb("ones3", [3, 128], bf16)
        neg_bf1, neg_bo1 = sb("neg_bf1", [F, 1]), sb("neg_bo1", [F, 1])
        left_f1, left_o1 = sb("left_f1", [F, 1]), sb("left_o1", [F, 1])
        left_split = sb("left_split", [F, 1])
        ident = sb("ident", [128, 128])
        zeros = sb("zeros", [128, ZN * F])
        weight = sb("weight", [TE, NTILES])
        src_col = sb("src_col", [TE, NTILES], i32)
        src_f = sb("src_f", [TE, NTILES])
        dump_i = sb("dump_i", [TE, T], i32)
        dump = sb("dump", [TE, T])
        not_after = sb("not_after", [TE, GE])

        dst_all = sb("dst_all", [TE, NTILES], i32)
        dst_idx = [sb(f"dst_idx{j}", [TE, T], i32) for j in range(U)]
        attr = [sb(f"attr{j}", [R, GE]) for j in range(U)]
        xg = [sb(f"xg{j}", [TE, T, F]) for j in range(U)]
        e1 = [sb(f"e1_{k}", [F, GE]) for k in range(2)]
        s1 = [sb(f"s1_{k}", [F, GE]) for k in range(2)]
        xt = [sb(f"xt{k}", [F, GE]) for k in range(2)]
        h = sb("h", [F, GE])
        mt = [sb(f"mt{k}", [F, GE]) for k in range(2)]
        msg = sb("msg", [128, RING * T * F])
        src_row = [sb(f"src_row{v}", [128, GE], i32) for v in range(VS)]
        SAME_AT = [TE * t * (t + 1) // 2 for t in range(T + 1)]
        same = [sb(f"same{k}", [TE, SAME_AT[T]]) for k in range(2)]
        rank = [sb(f"rank{k}", [TE, T]) for k in range(2)]
        dumped = [sb(f"dumped{k}", [TE, T]) for k in range(2)]
        agg_idx = [sb(f"agg_idx{v}", [TE, T], i32) for v in range(VS)]
        sums = [sb(f"sums{v}", [TE, T, F]) for v in range(VS)]

        xn, an, rows_out = ([msg[:, n * CN * F:(n + 1) * CN * F].rearrange("p (c f) -> p c f", c=CN)
                         for n in range(a, a + NS)] for a in (0, NS, 2 * NS))
        s2 = [sb(f"s2_{k}", [F, 512]) for k in range(2)]
        relu2 = sb("relu2", [F, 512])
        e2 = [sb(f"e2_{k}", [F, 512]) for k in range(3)]
        stats = sb("stats", [128, CN, 6])
        dmean = sb("dmean", [128, CN])
        msum = [sb(f"msum{k}", [128, CN]) for k in range(2)]
        m2 = sb("m2", [128, CN])
        var = [sb(f"var{k}", [128, CN]) for k in range(2)]
        rstd0 = [sb(f"rstd0_{k}", [128, CN]) for k in range(2)]
        newton = sb("newton", [128, CN])
        rstd = [sb(f"rstd{k}", [128, CN]) for k in range(2)]
        nmr = [sb(f"nmr{k}", [128, CN]) for k in range(2)]
        nmean = [sb(f"nmean{k}", [128, CN]) for k in range(2)]

        bank = [ctx.enter_context(nc.psum_tensor(f"bank{n}", [128, 512], f32)) for n in range(8)]
        xt_ps, h_ps, w_ps, m_ps, sum_ps, z1_ps = *bank[0:5], bank[5:7]
        c_ps = bank[7]
        z2_ps, y_ps = bank[0:3], bank[3:5]

        weights_in = sem("weights_in")
        edges_in = sem("edges_in")
        c3_in = sem("c3_in")
        dst_in = sem("dst_in")
        src_in = [sem(f"src_in{v}") for v in range(VS)]
        attr_in = [sem(f"attr_in{j}") for j in range(U)]
        xg_in = [sem(f"xg_in{j}") for j in range(U)]
        zeroed = sem("zeroed")
        added = sem("added")
        xn_in = [sem(f"xn_in{s}") for s in range(NS)]
        an_in = [sem(f"an_in{s}") for s in range(NS)]
        out_done = [sem(f"out_done{s}") for s in range(NS)]
        zeros_set = sem("zeros_set")
        pool_consts = sem("pool_consts")
        dve_consts = sem("dve_consts")
        left_ready = sem("left_ready")
        split_step = sem("split_step")
        c_parts_ready = sem("c_parts_ready")
        idx_ready = sem("idx_ready")
        gather_turns = sem("gather_turns")
        add_turns = sem("add_turns")
        z1_ready = sem("z1_ready")
        abs1_ready = sem("abs1_ready")
        e1_ready = sem("e1_ready")
        l1_ready = sem("l1_ready")
        s1_ready = sem("s1_ready")
        xtp_ready = sem("xtp_ready")
        xt_ready = sem("xt_ready")
        hp_ready = sem("hp_ready")
        h_ready = sem("h_ready")
        w_ready = sem("w_ready")
        mt_ready = sem("mt_ready")
        mp_ready = sem("mp_ready")
        msg_ready = sem("msg_ready")
        same_ready = sem("same_ready")
        dumped_ready = sem("dumped_ready")
        agg_idx_ready = sem("agg_idx_ready")
        sump_ready = sem("sump_ready")
        sums_ready = sem("sums_ready")
        z2_ready = sem("z2_ready")
        abs2_ready = sem("abs2_ready")
        e2_ready = sem("e2_ready")
        l2_ready = sem("l2_ready")
        s2_ready = sem("s2_ready")
        relu_ready = sem("relu_ready")
        y_ready = sem("y_ready")
        xy_ready = sem("xy_ready")
        stats_ready = sem("stats_ready")
        moments_ready = sem("moments_ready")
        square_ready = sem("square_ready")
        newton_turns = sem("newton_turns")
        newton_1_ready = sem("newton_1_ready")
        newton_2_ready = sem("newton_2_ready")
        var_ready = sem("var_ready")
        lnvar_ready = sem("lnvar_ready")
        rough_ready = sem("rough_ready")
        newton_3_ready = sem("newton_3_ready")
        rstd_ready = sem("rstd_ready")
        norm_ready = sem("norm_ready")
        rows_ready = sem("rows_ready")
        act_rows_ready = sem("act_rows_ready")
        normalise_turns = sem("normalise_turns")

        N_WEIGHTS = 9

        def batch(k, s, q, back):
            n = Q * s + q - back
            turns = n // (Q * NS)
            n -= turns * Q * NS
            return NS * (k + turns) + n // Q, n // Q, n % Q, Q * NS * (k + turns) + n

        SPLIT_Q = 1

        def s2_count(c, q):
            return 2 * c + (1, 1, 2)[q]

        def b_slot(s, q):
            return (Q * s + q) % 2

        def z_slot(s, q):
            return (Q * s + q) % 3

        def real(*at_batch):
            return not isinstance(at_batch[3], int) or at_batch[3] >= 0

        def node_loop(engine, step):
            for s in range(NS):
                for q in range(Q):
                    step(0, s, q)
            with engine.Fori(1, KN) as k:
                for s in range(NS):
                    for q in range(Q):
                        step(k, s, q)
            for q in range(Q):
                step(KN, 0, q)

        LAST = (KN, 0, Q - 1)
        REST = Q * NCH
        RS = 1

        block = ctx.enter_context(nc.Block())

        @block.sync
        def _(sp):
            sp.dma_start(dst_all[:, :], dstT).then_inc(dst_in, 16)
            for j in range(U):
                sp.dma_start(attr[j][:, :], attrT[:, j * GE:(j + 1) * GE]).then_inc(attr_in[j], 16)
            for t, a in ((w_f1, W_f1), (w_in, W_in2f), (w_f2, W_f2), (w_o1, W_o1), (w_o2, W_o2)):
                sp.dma_start(t[:, :], a).then_inc(weights_in, 16)
            sp.dma_start(bf1_col[:, :], b_f1.rearrange("(p a) -> p a", a=1)).then_inc(weights_in, 16)
            sp.dma_start(bo1_col[:, :], b_o1.rearrange("(p a) -> p a", a=1)).then_inc(weights_in, 16)
            sp.dma_start(bf2_col[:, :], b_f2.rearrange("(p a) -> p a", a=1)).then_inc(weights_in, 16)
            sp.dma_start(bo2_row[:, :], b_o2.rearrange("(a n) -> a n", a=1)).then_inc(weights_in, 16)
            sp.dma_start(weight[:, :], weightT).then_inc(edges_in, 16)
            sp.dma_start(src_col[:, :], srcT).then_inc(edges_in, 16)
            for v in range(VS):
                slot = (v + V0) % VS
                sp.dma_start(src_row[slot][:, :], src[v * GE:(v + 1) * GE].partition_broadcast(128)).then_inc(src_in[slot], 16)
            def next_front(i, j):
                sp.wait_ge(z1_ready, U * i + j + 1)
                sp.dma_start(attr[j][:, :], attrT[:, bass.ds((i + 1) * U * GE + j * GE, GE)]).then_inc(attr_in[j], 16)

            def next_back(s, b):
                m = V * s - V0 + b
                sp.wait_ge(same_ready, m + 1)
                sp.dma_start(src_row[b % VS][:, :],
                             src[bass.ds((m + VS) * GE, GE)].partition_broadcast(128)).then_inc(src_in[b % VS], 16)

            zero_ch = agg_dram[0:NZ * 128 * ZN, :].rearrange("(p c) f -> p (c f)", p=128)
            sp.wait_ge(zeros_set, 1)
            sp.dma_start(agg_dram[NZ * 128 * ZN:N + DUMP, :].rearrange("(p c) f -> p (c f)", c=ZR),
                         zeros[0:ZP, 0:ZR * F]).then_inc(zeroed, 16)

            def zero(n):
                sp.dma_start(zero_ch[:, bass.ds(n * ZN * F, ZN * F)], zeros[:, :]).then_inc(zeroed, 16)

            with sp.Fori(0, LEAD) as i:
                for j in range(U):
                    for n in range(j * (NZ // LEAD) // U, (j + 1) * (NZ // LEAD) // U):
                        zero(i * (NZ // LEAD) + n)
                    next_front(i, j)
            sp.wait_ge(c_parts_ready, 1)
            for t in range(T):
                for k in range(2):
                    sp.dma_start(c3[:, k, t, :], c_parts[0:1, k, :, :]).then_inc(c3_in, 16)

            def both(s, mix=MIX, fronts_next=U):
                for j, backs in mix:
                    if j < fronts_next:
                        next_front(LEAD + s, j)
                    for b in backs:
                        next_back(s, b)

            for b in FIRST_BACKS:
                next_back(0, b)
            both(0, FIRST_MIX)
            with sp.Fori(1, NM - 2) as s:
                both(s)
            both(NM - 2, fronts_next=UL)
            for b in range(LAST_BACKS - VS):
                next_back(NM - 1, b)

            def load_x(c, s):
                sp.dma_start(xn[s][:, :, :].rearrange("p c f -> p (c f)"),
                             x_ch[:, bass.ds(c * CN * F, CN * F)]).then_inc(xn_in[s], 16)

            def load_agg(c, s):
                sp.dma_start(an[s][:, :, :].rearrange("p c f -> p (c f)"),
                             agg_ch[:, bass.ds(c * CN * F, CN * F)]).then_inc(an_in[s], 16)

            def store(c, s):
                sp.dma_start(out_ch[:, bass.ds(c * CN * F, CN * F)],
                             rows_out[s][:, :, :].rearrange("p c f -> p (c f)")).then_inc(out_done[s], 16)

            def wait_rows(c):
                sp.wait_ge(rows_ready, c + 1)
                sp.wait_ge(act_rows_ready, c + 1)

            def step(c, s):
                sp.wait_ge(z2_ready, Q * (c + 1))
                if not isinstance(c, int) or c + 4 < NCH:
                    load_agg(c + 4, s)
                if not isinstance(c, int) or c >= 2:
                    wait_rows(c - 2)
                    store(c - 2, (s - 2) % NS)
                    if not isinstance(c, int) or c + 2 < NCH:
                        load_x(c + 2, (s + 2) % NS)

            sp.wait_ge(sump_ready, NG)
            for s in range(2):
                load_x(s, s)
            sp.wait_ge(added, 16 * NTILES)
            for s in range(2):
                load_agg(s, s)
            for s in range(2, NS):
                load_x(s, s)
                load_agg(s, s)
            for s in range(NS):
                step(s, s)
            with sp.Fori(1, KN - 1) as k:
                for s in range(NS):
                    step(NS * k + s, s)
            for s in range(NS):
                step(NS * (KN - 1) + s, s)
                if s == RS:
                    sp.dma_start(an[RS][0:TP, 0:TN, :].rearrange("p c f -> p (c f)"), rest(agg_dram)).then_inc(an_in[RS], 16)
            step(NCH - 1, 0)
            sp.dma_start(xn[RS][0:TP, 0:TN, :].rearrange("p c f -> p (c f)"), rest(x)).then_inc(xn_in[RS], 16)
            wait_rows(NCH - 2)
            store(NCH - 2, (NCH - 2) % NS)
            wait_rows(NCH - 1)
            store(NCH - 1, 0)
            wait_rows(NCH)
            sp.dma_start(rest(out), rows_out[RS][0:TP, 0:TN, :].rearrange("p c f -> p (c f)")).then_inc(out_done[RS], 16)
            for s in range(NS):
                sp.wait_ge(out_done[s], 16 * (KN + (s in (0, RS))))

        @block.gpsimd
        def _(pool):
            def gather(i, j, tiles):
                for t in tiles:
                    pool.indirect_dma_start(
                        out=xg[j][:, t, :], out_offset=None, in_=x,
                        in_offset=bass.IndirectOffsetOnAxis(ap=dst_idx[j][:, t:t + 1], axis=0),
                    ).then_inc(xg_in[j], 16)

            def ready_to_gather(i, j):
                pool.wait_ge(idx_ready, U * i + j + 1)
                wait(pool, xtp_ready, U * (i - 1) + j + 1)
                pool.sem_inc(gather_turns, 1)

            def add(s, b):
                m = V * s - V0 + b
                pool.wait_ge(agg_idx_ready, m + 1)
                pool.wait_ge(sums_ready, m + 1)
                wait(pool, added, 16 * T * m)
                pool.sem_inc(add_turns, 1)
                for t in range(T):
                    pool.indirect_dma_start(
                        out=agg_dram, in_=sums[b % VS][:, t, :], in_offset=None,
                        out_offset=bass.IndirectOffsetOnAxis(ap=agg_idx[b % VS][:, t:t + 1], axis=0),
                        compute_op=ALU.add,
                    ).then_inc(added, 16)

            nc.gpsimd.memset(ident[:, :], 0.0).then_inc(pool_consts, 1)
            nc.gpsimd.memset(not_after[:, :], 1.0).then_inc(pool_consts, 1)
            ready_to_gather(0, 0)
            gather(0, 0, range(T))
            pool.wait_ge(pool_consts, 2)
            pool.affine_select(out=ident[:, :], in_=ident[:, :], compare_op=ALU.not_equal, fill=1.0,
                               base=0, pattern=[[-1, 128]], channel_multiplier=1).then_inc(pool_consts, 1)
            pool.affine_select(out=not_after[:, :], in_=not_after[:, :], compare_op=ALU.is_ge, fill=0.0,
                               base=GE - TE, pattern=[[-1, GE]], channel_multiplier=1).then_inc(pool_consts, 1)
            pool.iota(dump_i[:, :], pattern=[[TE, T]], base=N, channel_multiplier=1).then_inc(pool_consts, 1)
            for j in range(1, U):
                ready_to_gather(0, j)
                gather(0, j, range(T))
            with pool.Fori(1, LEAD + 1) as i:
                for j in range(U):
                    ready_to_gather(i, j)
                    gather(i, j, range(T))
            pool.wait_ge(zeroed, 16 * (NZ + 1))
            pool.sem_inc(add_turns, 1)

            def add_and_gather(s, b0=0, fronts_next=U):
                for b in range(b0, V):
                    add(s, b)
                    from_g, to_g = ((n - b0) * U * T // (V - b0) for n in (b, b + 1))
                    for g in range(from_g, min(to_g, fronts_next * T)):
                        if g % T == 0:
                            ready_to_gather(LEAD + s + 1, g // T)
                        gather(LEAD + s + 1, g // T, (g % T,))

            add_and_gather(0, V0)
            with pool.Fori(1, NM - 2) as s:
                add_and_gather(s)
            add_and_gather(NM - 2, fronts_next=UL)
            for b in range(LAST_BACKS):
                add(NM - 1, b)

            def normalise(c, s, stores, P=128, C=CN, others=AR):
                r0, nt = rstd0[s % 2][0:P, 0:C], newton[0:P, 0:C]
                pool.wait_ge(rough_ready, c + 1)
                wait(pool, act_rows_ready, c - 1)
                pool.sem_inc(newton_turns, 1)
                nc.gpsimd.tensor_tensor(nt, r0, r0, ALU.mult).then_inc(newton_1_ready, 1)
                nc.gpsimd.tensor_scalar(nmean[s % 2][0:P, 0:C], msum[s % 2][0:P, 0:C], -0.5, None, ALU.mult)
                pool.wait_ge(newton_1_ready, c + 1)
                pool.sem_inc(newton_turns, 1)
                nc.gpsimd.tensor_tensor(nt, nt, var[s % 2][0:P, 0:C], ALU.mult).then_inc(newton_2_ready, 1)
                pool.wait_ge(newton_2_ready, c + 1)
                pool.sem_inc(newton_turns, 1)
                nc.gpsimd.tensor_scalar(nt, nt, -0.5 / F, 1.5, ALU.mult, ALU.add).then_inc(newton_3_ready, 1)
                pool.wait_ge(newton_3_ready, c + 1)
                pool.sem_inc(newton_turns, 1)
                nc.gpsimd.tensor_tensor(rstd[s % 2][0:P, 0:C], nt, r0, ALU.mult).then_inc(rstd_ready, 1)
                wait(pool, out_done[s], 16 * stores)
                pool.wait_ge(rstd_ready, c + 1)
                pool.sem_inc(normalise_turns, 1)
                nc.gpsimd.tensor_tensor(nmr[s % 2][0:P, 0:C], nmean[s % 2][0:P, 0:C], rstd[s % 2][0:P, 0:C],
                                        ALU.mult).then_inc(norm_ready, 1)
                for r in range(C - others):
                    last = nc.gpsimd.tensor_scalar(rows_out[s][0:P, r, :], xn[s][0:P, r, :], nmean[s % 2][0:P, r:r + 1],
                                                   rstd[s % 2][0:P, r:r + 1], ALU.add, ALU.mult)
                last.then_inc(rows_ready, 1)

            for s in range(NS):
                normalise(s, s, 0)
            with pool.Fori(1, KN) as k:
                for s in range(NS):
                    normalise(NS * k + s, s, k)
            normalise(NCH - 1, 0, KN, others=AR_LAST)
            normalise(NCH, RS, KN, TP, TN, AR_REST)

        @block.tensor
        def _(pe):
            pe.wait_ge(weights_in, 16 * N_WEIGHTS)
            pe.wait_ge(dve_consts, 1)
            nc.tensor.matmul(c_ps[:, 3 * F:3 * F + 1], w_f2[:, :], left_f1[:, :], start=True, stop=True)
            nc.tensor.matmul(c_ps[0:1, 0:F], left_o1[:, :], w_o2[:, :], start=True, stop=True)
            nc.tensor.matmul(c_ps[0:1, F:2 * F], left_split[:, :], w_o2[:, :], start=True, stop=True).then_inc(left_ready, 1)
            pe.wait_ge(pool_consts, 5)

            def filter_in(i, j):
                n = U * i + j
                pe.wait_ge(attr_in[j], 16 * (i + 1))
                wait(pe, s1_ready, n - 1)
                nc.tensor.matmul(z1_ps[j % 2][:, 0:GE], w_f1[:, :], attr[j][:, :], start=True, stop=True).then_inc(z1_ready, 1)
                pe.wait_ge(xg_in[j], 16 * T * (i + 1))
                wait(pe, xt_ready, n)
                for t in range(T):
                    last = nc.tensor.transpose(xt_ps[:, t * TE:(t + 1) * TE], xg[j][:, t, :], ident[0:TE, 0:TE])
                last.then_inc(xtp_ready, 1)

            def message(i, j):
                n = U * i + j
                pe.wait_ge(xt_ready, n + 1)
                wait(pe, h_ready, n)
                nc.tensor.matmul(h_ps[:, 0:GE], w_in[:, :], xt[j % 2][:, :], start=True, stop=True).then_inc(hp_ready, 1)
                wait(pe, mt_ready, n)
                pe.wait_ge(s1_ready, n + 1)
                nc.tensor.matmul(w_ps[:, 0:GE], w_f2[:, :], s1[j % 2][:, :], start=True, stop=True).then_inc(w_ready, 1)

            def message_out(i, j):
                n = U * i + j
                pe.wait_ge(mt_ready, n + 1)
                wait(pe, msg_ready, n)
                for t in range(T):
                    last = nc.tensor.matmul(m_ps[0:TE, t * F:(t + 1) * F], mt[j % 2][:, t * TE:(t + 1) * TE],
                                            w_o1[:, :], start=True, stop=True)
                last.then_inc(mp_ready, 1)

            def sum_group(s, b):
                m = V * s - V0 + b
                pe.wait_ge(same_ready, m + 1)
                pe.wait_ge(msg_ready, m + 1)
                wait(pe, sums_ready, m)
                for t in range(T):
                    for u in range(t, T):
                        last = nc.tensor.matmul(
                            sum_ps[0:TE, t * F:(t + 1) * F],
                            same[b % 2][:, SAME_AT[u] + t * TE:SAME_AT[u] + (t + 1) * TE],
                            msg[0:TE, bass.ds((m % RING) * (T * F) + u * F, F)], start=(u == t), stop=(u == T - 1))
                last.then_inc(sump_ready, 1)

            def front(i, j, first=False, last=False):
                if not last:
                    filter_in(*after(i, j))
                message(i, j)
                if not first:
                    message_out(*before(i, j))

            filter_in(0, 0)
            for j in range(U):
                front(0, j, first=(j == 0))
            with pe.Fori(1, LEAD) as i:
                for j in range(U):
                    front(i, j)

            def both(s, mix=MIX, last=False):
                for j, backs in mix:
                    front(LEAD + s, j, last=(last and j == UL - 1))
                    for b in backs:
                        sum_group(s, b)

            for b in FIRST_BACKS:
                sum_group(0, b)
            both(0, FIRST_MIX)
            with pe.Fori(1, NM - 1) as s:
                both(s)
            both(NM - 1, LAST_MIX, last=True)
            message_out(NI - 1, UL - 1)
            sum_group(NM - 1, LAST_BACKS - 1)

            pe.wait_ge(sums_ready, NG)

            pe.wait_ge(c3_in, 16 * 2 * T)

            def transpose_agg(c, s, q, b, k, P=128, tiles=4):
                pe.wait_ge(an_in[s], 16 * (k + 1))
                if q == SPLIT_Q:
                    wait(pe, relu_ready, c)
                else:
                    wait(pe, s2_ready, s2_count(c - 1, q))
                for t in range(tiles):
                    last = nc.tensor.transpose(z2_ps[z_slot(s, q)][:, t * P:(t + 1) * P], an[s][0:P, 4 * q + t, :],
                                               ident[0:P, 0:P])
                last.then_inc(z2_ready, 1)

            def update(c, s, q, b, P=128, tiles=4):
                split = q == SPLIT_Q
                if split:
                    pe.wait_ge(l2_ready, b + 1)
                    pe.wait_ge(relu_ready, c + 1)
                else:
                    pe.wait_ge(s2_ready, s2_count(c, q))
                wait(pe, xy_ready, b - 1)
                y = y_ps[b_slot(s, q)]
                nc.tensor.matmul(y[0:P, 0:tiles * F], ones3[:, 0:P],
                                 c3[:, int(split), 0:tiles, :].rearrange("p t f -> p (t f)"),
                                 start=True, stop=False, skip_group_check=True)
                parts = (relu2, e2[z_slot(s, q)]) if split else (s2[q // 2],)
                for part in parts:
                    for t in range(tiles):
                        last = nc.tensor.matmul(y[0:P, t * F:(t + 1) * F], part[:, t * P:(t + 1) * P], w_o2[:, :], start=False,
                                                stop=(part is parts[-1] and t == tiles - 1), skip_group_check=True)
                last.then_inc(y_ready, 1)

            def step(k, s, q):
                transpose_agg(*batch(k, s, q, 0), k)
                if real(*batch(k, s, q, 2)):
                    update(*batch(k, s, q, 2))

            node_loop(pe, step)
            the_rest = (NCH, RS, 0, REST)
            transpose_agg(*the_rest, KN, TP, TN)
            update(*batch(*LAST, 1))
            update(*batch(*LAST, 0))
            update(*the_rest, TP, TN)

        @block.scalar
        def _(act):
            act.preload_act_table_set("natural_log_exp_and_others")

            act.wait_ge(weights_in, 16 * N_WEIGHTS)

            def abs1(i, j):
                n = U * i + j
                act.wait_ge(z1_ready, n + 1)
                wait(act, s1_ready, n - 1)
                nc.scalar.activation(e1[j % 2][:, :], z1_ps[j % 2][:, 0:GE], ACT.Abs, bias=bf1_col[:, :]).then_inc(abs1_ready, 1)

            def exp1(i, j):
                act.wait_ge(abs1_ready, U * i + j + 1)
                nc.scalar.activation(e1[j % 2][:, :], e1[j % 2][:, :], ACT.Exp, scale=-1.0).then_inc(e1_ready, 1)

            def copy_xt(i, j):
                n = U * i + j
                act.wait_ge(xtp_ready, n + 1)
                wait(act, hp_ready, n - 1)
                nc.scalar.activation(xt[j % 2][:, :], xt_ps[:, 0:GE], ACT.Copy).then_inc(xt_ready, 1)

            def copy_h(i, j):
                n = U * i + j
                act.wait_ge(hp_ready, n + 1)
                wait(act, mt_ready, n)
                nc.scalar.activation(h[:, :], h_ps[:, 0:GE], ACT.Copy).then_inc(h_ready, 1)

            def ln1(i, j):
                act.wait_ge(e1_ready, U * i + j + 1)
                nc.scalar.activation(e1[j % 2][:, :], e1[j % 2][:, :], ACT.Ln, bias=1.0).then_inc(l1_ready, 1)

            def copy_sums(s, b):
                m = V * s - V0 + b
                act.wait_ge(sump_ready, m + 1)
                wait(act, added, 16 * T * (m - VS + 1))
                nc.scalar.activation(sums[b % VS][:, :, :].rearrange("p t f -> p (t f)"), sum_ps[0:TE, :],
                                     ACT.Copy).then_inc(sums_ready, 1)

            def front(i, j):
                abs1(*after(i, j))
                exp1(*after(i, j))
                copy_xt(*after(i, j))
                ln1(*after(i, j))
                copy_h(i, j)

            def both(s, mix=MIX, last=False):
                for j, backs in mix:
                    if last and j == UL - 1:
                        copy_h(LEAD + s, j)
                    else:
                        front(LEAD + s, j)
                    for b in backs:
                        copy_sums(s, b)

            abs1(0, 0)
            exp1(0, 0)
            copy_xt(0, 0)
            ln1(0, 0)
            for j in range(U):
                front(0, j)
            with act.Fori(1, LEAD) as i:
                for j in range(U):
                    front(i, j)
            for b in FIRST_BACKS:
                copy_sums(0, b)
            both(0, FIRST_MIX)
            with act.Fori(1, NM - 1) as s:
                both(s)
            both(NM - 1, LAST_MIX, last=True)
            copy_sums(NM - 1, LAST_BACKS - 1)

            def abs2(c, s, q, b, W=512):
                z = z_slot(s, q)
                act.wait_ge(z2_ready, b + 1)
                if q == SPLIT_Q:
                    wait(act, y_ready, b - 2)
                else:
                    wait(act, s2_ready, s2_count(c - 1, q))
                nc.scalar.activation(e2[z][:, 0:W], z2_ps[z][:, 0:W], ACT.Abs, bias=bo1_col[:, :]).then_inc(abs2_ready, 1)

            def exp2(c, s, q, b, W=512):
                z = z_slot(s, q)
                act.wait_ge(abs2_ready, b + 1)
                nc.scalar.activation(e2[z][:, 0:W], e2[z][:, 0:W], ACT.Exp, scale=-1.0).then_inc(e2_ready, 1)

            def relu(c, s, q, b):
                nc.scalar.activation(relu2[:, :], z2_ps[z_slot(s, q)][:, :], ACT.Relu, bias=bo1_col[:, :]).then_inc(relu_ready, 1)

            def ln2(c, s, q, b, W=512):
                z = z_slot(s, q)
                act.wait_ge(e2_ready, b + 1)
                nc.scalar.activation(e2[z][:, 0:W], e2[z][:, 0:W], ACT.Ln, bias=1.0).then_inc(l2_ready, 1)

            def rough_rstd(c, s, P=128, C=CN):
                r0 = rstd0[s % 2][0:P, 0:C]
                act.wait_ge(var_ready, c + 1)
                nc.scalar.activation(r0, var[s % 2][0:P, 0:C], ACT.Ln, scale=1.0 / F).then_inc(lnvar_ready, 1)
                act.wait_ge(lnvar_ready, c + 1)
                nc.scalar.activation(r0, r0, ACT.Exp, scale=-0.5).then_inc(rough_ready, 1)

            def last_rows(c, s, stores, P=128, C=CN, mine=AR):
                wait(act, out_done[s], 16 * stores)
                act.wait_ge(norm_ready, c + 1)
                for r in range(C - mine, C):
                    last = nc.scalar.activation(rows_out[s][0:P, r, :], xn[s][0:P, r, :], ACT.Identity,
                                                bias=nmr[s % 2][0:P, r:r + 1], scale=rstd[s % 2][0:P, r:r + 1])
                last.then_inc(act_rows_ready, 1)

            def step(k, s, q):
                for stage, back in ((abs2, 0), (ln2, 1), (exp2, 0)):
                    if real(*batch(k, s, q, back)):
                        stage(*batch(k, s, q, back))
                if q == SPLIT_Q:
                    relu(*batch(k, s, q, 0))
                c, cs, cq, b = batch(k, s, q, 4)
                if cq == Q - 1 and real(c, cs, cq, b):
                    rough_rstd(c, cs)
                c, cs, cq, b = batch(k, s, q, 7)
                if cq == Q - 1 and real(c, cs, cq, b):
                    last_rows(c, cs, k if Q * s + q >= 7 else k - 1)

            node_loop(act, step)
            the_rest = (NCH, RS, 0, REST)
            abs2(*the_rest, TP * TN)
            ln2(*batch(*LAST, 0))
            exp2(*the_rest, TP * TN)
            rough_rstd(NCH - 2, NS - 1)
            ln2(*the_rest, TP * TN)
            last_rows(NCH - 3, NS - 2, KN - 1)
            rough_rstd(NCH - 1, 0)
            rough_rstd(NCH, RS, TP, TN)
            last_rows(NCH - 2, NS - 1, KN - 1)
            last_rows(NCH - 1, 0, KN, mine=AR_LAST)
            last_rows(NCH, RS, KN, TP, TN, AR_REST)

        @block.vector
        def _(dve):
            dve.wait_ge(dst_in, 16)
            for j in range(U):
                nc.vector.tensor_copy(dst_idx[j][:, :], dst_all[:, j * T:(j + 1) * T]).then_inc(idx_ready, 1)
            nc.vector.memset(zeros[:, :], 0.0).then_inc(zeros_set, 1)
            nc.vector.memset(ones3[:, :], 1.0)
            dve.wait_ge(weights_in, 16 * N_WEIGHTS)
            nc.vector.tensor_scalar(neg_bf1[:, :], bf1_col[:, :], -1.0, None, ALU.mult)
            nc.vector.tensor_scalar(neg_bo1[:, :], bo1_col[:, :], -1.0, None, ALU.mult)
            nc.vector.memset(left_split[:, :], -LOG2)
            nc.vector.tensor_scalar(left_f1[:, :], bf1_col[:, :], -LOG2, None, ALU.add)
            nc.vector.tensor_scalar(left_o1[:, :], bo1_col[:, :], -LOG2, None, ALU.add).then_inc(dve_consts, 1)
            dve.wait_ge(left_ready, 1)
            nc.vector.tensor_tensor(cf_col[:, :], c_ps[:, 3 * F:3 * F + 1], bf2_col[:, :], ALU.add).then_inc(dve_consts, 1)
            nc.vector.tensor_tensor(c_rows[:, 0, :], c_ps[0:1, 0:F], bo2_row[:, :], ALU.add)
            nc.vector.tensor_tensor(c_rows[:, 1, :], c_ps[0:1, F:2 * F], bo2_row[:, :], ALU.add).then_inc(split_step, 1)
            for part in range(3):
                dve.wait_ge(split_step, 1 + 2 * part)
                nc.vector.tensor_copy(c_parts[:, :, part, :], c_rows[:, :, :]).then_inc(
                    c_parts_ready if part == 2 else split_step, 1)
                if part < 2:
                    dve.wait_ge(split_step, 2 + 2 * part)
                    nc.vector.tensor_tensor(c_rows[:, :, :], c_rows[:, :, :], c_parts[:, :, part, :],
                                            ALU.subtract).then_inc(split_step, 1)
            dve.wait_ge(edges_in, 16 * 2)
            nc.vector.tensor_copy(src_f[:, :], src_col[:, :]).then_inc(dve_consts, 1)
            dve.wait_ge(pool_consts, 5)
            nc.vector.tensor_copy(dump[:, :], dump_i[:, :]).then_inc(dve_consts, 1)
            dve.wait_ge(dve_consts, 4)

            def next_indices(i, j):
                dve.wait_ge(xg_in[j], 16 * T * (i + 1))
                nc.vector.tensor_copy(dst_idx[j][:, :], dst_all[:, bass.ds(T * (U * i + U + j), T)]).then_inc(idx_ready, 1)

            def softplus1(i, j):
                n = U * i + j
                dve.wait_ge(l1_ready, n + 1)
                wait(dve, w_ready, n - 1)
                nc.vector.scalar_tensor_tensor(s1[j % 2][:, :], z1_ps[j % 2][:, 0:GE], neg_bf1[:, :], e1[j % 2][:, :],
                                               ALU.max, ALU.add).then_inc(s1_ready, 1)

            def message(i, j):
                n = U * i + j
                dve.wait_ge(h_ready, n + 1)
                dve.wait_ge(w_ready, n + 1)
                wait(dve, mp_ready, n - 1)
                nc.vector.scalar_tensor_tensor(mt[j % 2][:, :], w_ps[:, 0:GE], cf_col[:, :], h[:, :],
                                               ALU.add, ALU.mult).then_inc(mt_ready, 1)

            def weigh(i, j):
                n = U * i + j
                dve.wait_ge(mp_ready, n + 1)
                for t in range(T):
                    last = nc.vector.tensor_scalar(
                        msg[0:TE, bass.ds((n % RING) * (T * F) + t * F, F)], m_ps[0:TE, t * F:(t + 1) * F],
                        weight[:, bass.ds(T * n + t, 1)], None, ALU.mult)
                last.then_inc(msg_ready, 1)

            def mark(s, b):
                m = V * s - V0 + b
                dve.wait_ge(src_in[b % VS], 16 * (V // VS * s + (b - V0) // VS + 1))
                wait(dve, sump_ready, m - 1)
                for u in range(T):
                    last = nc.vector.scalar_tensor_tensor(
                        same[b % 2][:, SAME_AT[u]:SAME_AT[u + 1]], src_row[b % VS][0:TE, 0:TE * (u + 1)],
                        src_f[:, bass.ds(T * m + u, 1)], not_after[:, GE - TE * (u + 1):GE],
                        ALU.is_equal, ALU.mult, accum_out=rank[b % 2][:, u:u + 1])
                last.then_inc(same_ready, 1)

            def index(s, b):
                m = V * s - V0 + b
                dve.wait_ge(same_ready, m + 1)
                nc.vector.scalar_tensor_tensor(dumped[b % 2][:, :], rank[b % 2][:, :], 1.5, dump[:, :],
                                               ALU.is_gt, ALU.mult).then_inc(dumped_ready, 1)
                dve.wait_ge(dumped_ready, m + 1)
                wait(dve, added, 16 * T * (m - VS + 1))
                nc.vector.tensor_tensor(agg_idx[b % VS][:, :], dumped[b % 2][:, :], src_f[:, bass.ds(T * m, T)],
                                        ALU.max).then_inc(agg_idx_ready, 1)

            def front(i, j, first=False, fronts_next=U):
                if j < fronts_next:
                    next_indices(i, j)
                if fronts_next or j < UL - 1:
                    softplus1(*after(i, j))
                message(i, j)
                if not first:
                    weigh(*before(i, j))

            def both(s, mix=MIX, fronts_next=U):
                for j, backs in mix:
                    for b in backs:
                        mark(s, b)
                    front(LEAD + s, j, fronts_next=fronts_next)
                    for b in backs:
                        index(s, b)

            softplus1(0, 0)
            for j in range(U):
                front(0, j, first=(j == 0))
            with dve.Fori(1, LEAD) as i:
                for j in range(U):
                    front(i, j)
            for b in FIRST_BACKS:
                mark(0, b)
                index(0, b)
            both(0, FIRST_MIX)
            with dve.Fori(1, NM - 2) as s:
                both(s)
            both(NM - 2, fronts_next=UL)
            both(NM - 1, LAST_MIX, fronts_next=0)
            mark(NM - 1, LAST_BACKS - 1)
            weigh(NI - 1, UL - 1)
            index(NM - 1, LAST_BACKS - 1)

            def softplus2(c, s, q, b, W=512):
                if q == SPLIT_Q:
                    return
                z = z_slot(s, q)
                dve.wait_ge(l2_ready, b + 1)
                wait(dve, y_ready, b - 2)
                nc.vector.scalar_tensor_tensor(s2[q // 2][:, 0:W], z2_ps[z][:, 0:W], neg_bo1[:, :], e2[z][:, 0:W],
                                               ALU.max, ALU.add).then_inc(s2_ready, 1)

            def residual(c, s, q, b, loads, P=128, tiles=4):
                rows = xn[s][0:P, 4 * q:4 * q + tiles, :]
                if q == 0:
                    dve.wait_ge(xn_in[s], 16 * loads)
                dve.wait_ge(y_ready, b + 1)
                nc.vector.tensor_tensor(rows, y_ps[b_slot(s, q)][0:P, 0:tiles * F].rearrange("p (t f) -> p t f", t=tiles),
                                        rows, ALU.add).then_inc(xy_ready, 1)

            def statistics(c, s, q, b, P=128, tiles=4):
                dve.wait_ge(xy_ready, b + 1)
                for r in range(4 * q, 4 * q + tiles):
                    last = nc.vector.bn_stats(stats[0:P, r, :], xn[s][0:P, r, :])
                last.then_inc(stats_ready, 1)

            def moments(c, s, P=128, C=CN):
                mean_e, m2_e, mean_o, m2_o = (stats[0:P, 0:C, m] for m in (1, 2, 4, 5))
                dve.wait_ge(stats_ready, Q * (c + 1) if P == 128 else REST + 1)
                wait(dve, norm_ready, c - 1)
                nc.vector.tensor_tensor(dmean[0:P, 0:C], mean_e, mean_o, ALU.subtract)
                nc.vector.tensor_tensor(msum[s % 2][0:P, 0:C], mean_e, mean_o, ALU.add)
                nc.vector.scalar_tensor_tensor(m2[0:P, 0:C], m2_e, F * EPS, m2_o, ALU.add, ALU.add).then_inc(moments_ready, 1)

            def square_dmean(c, s, P=128, C=CN):
                dve.wait_ge(moments_ready, c + 1)
                nc.vector.tensor_tensor(dmean[0:P, 0:C], dmean[0:P, 0:C], dmean[0:P, 0:C], ALU.mult).then_inc(square_ready, 1)

            def variance(c, s, P=128, C=CN):
                dve.wait_ge(square_ready, c + 1)
                nc.vector.scalar_tensor_tensor(var[s % 2][0:P, 0:C], dmean[0:P, 0:C], F / 4.0, m2[0:P, 0:C],
                                               ALU.mult, ALU.add).then_inc(var_ready, 1)

            def chunk_work(k, s, q, parts):
                for back, part in parts:
                    c, cs, cq, b = batch(k, s, q, back)
                    if cq == Q - 1 and real(c, cs, cq, b):
                        part(c, cs)

            def step(k, s, q):
                if real(*batch(k, s, q, 1)):
                    softplus2(*batch(k, s, q, 1))
                chunk_work(k, s, q, ((3, moments),))
                if real(*batch(k, s, q, 2)):
                    turn = k if Q * s + q >= 2 else k - 1
                    residual(*batch(k, s, q, 2), turn + 1)
                chunk_work(k, s, q, ((3, square_dmean),))
                if real(*batch(k, s, q, 2)):
                    statistics(*batch(k, s, q, 2))
                chunk_work(k, s, q, ((3, variance),))

            node_loop(dve, step)
            the_rest, last = (NCH, RS, 0, REST), (NCH - 1, 0)
            softplus2(*batch(*LAST, 0))
            residual(*batch(*LAST, 1), KN + 1)
            statistics(*batch(*LAST, 1))
            softplus2(*the_rest, TP * TN)
            residual(*batch(*LAST, 0), KN + 1)
            statistics(*batch(*LAST, 0))
            for part in (moments, square_dmean, variance):
                part(*last)
            residual(*the_rest, KN + 1, TP, TN)
            statistics(*the_rest, TP, TN)
            for part in (moments, square_dmean, variance):
                part(NCH, RS, TP, TN)


def kernel(x, src, dst, edge_attr_20, edge_weight, L0_gnn_W_in2f, L0_gnn_W_f1, L0_gnn_b_f1, L0_gnn_W_f2,
           L0_gnn_b_f2, L0_gnn_W_o1, L0_gnn_b_o1, L0_gnn_W_o2, L0_gnn_b_o2):
    import numpy as _np
    import concourse.bacc as _bacc
    from concourse import mybir as _mybir
    from concourse.bass_utils import run_bass_kernel_spmd as _run

    TILE, GROUP = 128, 512
    E = src.shape[0]
    PAD = -E % GROUP

    def padded(a, value=0):
        return _np.pad(_np.asarray(a), [(0, 0)] * (_np.ndim(a) - 1) + [(0, PAD)], constant_values=value)

    def tiled(a):
        return _np.ascontiguousarray(a.reshape(-1, TILE).T)

    src = padded(src, x.shape[0])
    arrays = {
        "x": x, "dstT": tiled(padded(dst)), "src": src, "srcT": tiled(src),
        "attrT": padded(_np.asarray(edge_attr_20).T), "weightT": tiled(padded(_np.asarray(edge_weight).reshape(-1))),
        "W_in2f": L0_gnn_W_in2f, "W_f1": L0_gnn_W_f1, "b_f1": L0_gnn_b_f1, "W_f2": L0_gnn_W_f2,
        "b_f2": L0_gnn_b_f2, "W_o1": L0_gnn_W_o1, "b_o1": L0_gnn_b_o1, "W_o2": L0_gnn_W_o2, "b_o2": L0_gnn_b_o2,
    }
    arrays = {k: _np.ascontiguousarray(v) for k, v in arrays.items()}
    nc = _bacc.Bacc("TRN2", target_bir_lowering=False, num_devices=1)
    args = [nc.dram_tensor(k, a.shape, _mybir.dt.from_np(a.dtype), kind="ExternalInput").ap()
            for k, a in arrays.items()]
    out = nc.dram_tensor("out", arrays["x"].shape, _mybir.dt.float32, kind="ExternalOutput").ap()
    gnn_resnorm_kernel(nc, *args, out)
    r = _run(nc, [arrays], core_ids=[0])
    return r.results[0]["out"]
```
